# Optimizing a Trainium2 kernel written in Bass

```python
import numpy as np
import jax
import jax.numpy as jnp

def _softmax(x, axis=-1):
    return jax.nn.softmax(x, axis=axis)

def _gelu(x):
    return jax.nn.gelu(x, approximate=True)

def _silu(x):
    return jax.nn.silu(x)

def _sigmoid(x):
    return jax.nn.sigmoid(x)

def _layernorm(x, axis=-1, eps=1e-05):
    m = jnp.mean(x, axis=axis, keepdims=True)
    v = jnp.var(x, axis=axis, keepdims=True)
    return (x - m) / jnp.sqrt(v + eps)

def _scatter_add(tgt, idx, src, axis=0):
    return tgt.at[idx].add(src)

def _segment_sum(src, seg, n):
    return jax.ops.segment_sum(src, seg, n)
kernel_name = 'mk_adaln_attn_ffn_d1_seqx_r8_6cc4bd'

def setup_inputs(seed: int=0):
    np.random.seed(seed)
    _w = jnp.asarray

    def _rec_inputs():
        import jax
        import jax.numpy as jnp
        _rk = jax.random.key(seed)
        x = -0.0003929 + 0.9999 * jax.random.normal(jax.random.fold_in(_rk, 1), (128, 32, 512), jnp.float32)
        _lenS = 32 - jax.random.randint(jax.random.fold_in(_rk, 7), (128,), 0, max(1, 32 // 4) + 1, jnp.int32)
        _lenS2 = 32 - jax.random.randint(jax.random.fold_in(_rk, 8), (128,), 0, max(1, 32 // 4) + 1, jnp.int32)
        itok_B_78_3631 = jax.random.randint(jax.random.fold_in(_rk, 11), (128,), 78, 454, jnp.int32)
        itok_B_0_7 = jax.random.randint(jax.random.fold_in(_rk, 12), (128,), 0, 8, jnp.int32)
        itok_B_2182_4065 = jax.random.randint(jax.random.fold_in(_rk, 14), (128,), 2182, 4066, jnp.int32)
        return (x, itok_B_78_3631, itok_B_0_7, itok_B_2182_4065, _lenS)
    x, itok_B_78_3631, itok_B_0_7, itok_B_2182_4065, _lenS = _rec_inputs()

    def _L0_cond_setup():
        import math
        import jax, jax.numpy as jnp
        import numpy as np
        B, H, N, L = (16, 32, 64, 512)
        DT_MIN, DT_MAX = (0.001, 0.1)

        def _get_kernel(log_dt, C, log_A_real, A_imag, length):
            dt = jnp.exp(log_dt)
            Cc = C[..., 0] + 1j * C[..., 1]
            A = -jnp.exp(log_A_real) + 1j * A_imag
            dtA = A * dt[:, None]
            Ct = Cc * (jnp.exp(dtA) - 1.0) / A
            P = dtA[:, :, None] * jnp.arange(length, dtype=jnp.float32)
            K = 2.0 * jnp.einsum('hn,hnl->hl', Ct, jnp.exp(P)).real
            return K
        key = jax.random.key(seed)
        ks = jax.random.split(key, 5)
        u = jax.random.normal(ks[0], (B, H, L), dtype=jnp.float32)
        log_dt = jax.random.uniform(ks[1], (H,), dtype=jnp.float32) * (math.log(DT_MAX) - math.log(DT_MIN)) + math.log(DT_MIN)
        C = jax.random.normal(ks[2], (H, N, 2), dtype=jnp.float32)
        log_A_real = jnp.log(0.5 * jnp.ones((H, N), dtype=jnp.float32))
        A_imag = math.pi * jnp.broadcast_to(jnp.arange(N, dtype=jnp.float32), (H, N))
        D = jax.random.normal(ks[3], (H,), dtype=jnp.float32)
        length = jax.random.randint(ks[4], (B,), 1, L + 1, dtype=jnp.int32)
        return {'u': u, 'log_dt': log_dt, 'C': C, 'log_A_real': log_A_real, 'A_imag': A_imag, 'D': D, 'length': length}
    _L0_cond_all = _L0_cond_setup()
    _L0_cond_in = {k: v for k, v in _L0_cond_all.items() if k in ('log_dt', 'C', 'log_A_real', 'A_imag', 'D')}
    del _L0_cond_all

    def _L0_attn_setup():
        import jax, jax.numpy as jnp
        import numpy as np
        N_HEADS = 32
        N_KV_HEADS = 16
        N_EMBD = 512
        HEAD_DIM = N_EMBD // N_HEADS
        GROUPS = N_HEADS // N_KV_HEADS
        KV_DIM = N_KV_HEADS * HEAD_DIM
        SCALE = 1.0 / np.sqrt(np.float32(N_HEADS))
        key = jax.random.key(seed)
        ks = jax.random.split(key, 4)
        B, T, C = (1, 256, N_EMBD)
        s = 1.0 / np.sqrt(np.float32(C))
        return {'x': jax.random.normal(ks[0], (B, T, C), dtype=jnp.float32), 'Wq': jax.random.normal(ks[1], (C, C), dtype=jnp.float32) * s, 'bq': jnp.zeros((C,), dtype=jnp.float32), 'Wk': jax.random.normal(ks[2], (KV_DIM, C), dtype=jnp.float32) * s, 'bk': jnp.zeros((KV_DIM,), dtype=jnp.float32), 'Wv': jax.random.normal(ks[3], (KV_DIM, C), dtype=jnp.float32) * s, 'bv': jnp.zeros((KV_DIM,), dtype=jnp.float32)}
    _L0_attn_all = _L0_attn_setup()
    _L0_attn_in = {k: v for k, v in _L0_attn_all.items() if k in ('Wq', 'bq', 'Wk', 'bk', 'Wv', 'bv')}
    del _L0_attn_all

    def _L0_cond2_setup():
        import jax, jax.numpy as jnp
        import numpy as np
        SESSION_CHANNELS = [128, 160, 192, 224, 240, 248, 252, 32]
        N_SESS = len(SESSION_CHANNELS)
        B, MAX_C, MAX_T = (16, 32, 512)
        HID, N_SRC = (64, 32)
        key = jax.random.key(seed)
        ks = jax.random.split(key, 7)
        session_ids = jax.random.randint(ks[0], (B,), 0, N_SESS)
        chan_table = jnp.asarray(SESSION_CHANNELS)
        channel_counts = chan_table[session_ids]
        seq_lens = jax.random.randint(ks[1], (B,), MAX_T // 2, MAX_T + 1)
        x = jax.random.normal(ks[2], (B, MAX_C, MAX_T), jnp.float32)
        cmask = (jnp.arange(MAX_C)[None, :] < channel_counts[:, None]).astype(x.dtype)
        tmask = (jnp.arange(MAX_T)[None, :] < seq_lens[:, None]).astype(x.dtype)
        x = x * cmask[:, :, None] * tmask[:, None, :]
        lim1 = 1.0 / np.sqrt(MAX_C)
        W_sess = jax.random.uniform(ks[3], (N_SESS, MAX_C, HID), jnp.float32, -lim1, lim1)
        b_sess = jax.random.uniform(ks[4], (N_SESS, HID), jnp.float32, -lim1, lim1)
        lim2 = 1.0 / np.sqrt(HID)
        W2 = jax.random.uniform(ks[5], (HID, N_SRC), jnp.float32, -lim2, lim2)
        b2 = jax.random.uniform(ks[6], (N_SRC,), jnp.float32, -lim2, lim2)
        return dict(x=x, session_ids=session_ids, channel_counts=channel_counts, seq_lens=seq_lens, W_sess=W_sess, b_sess=b_sess, W2=W2, b2=b2)
    _L0_cond2_all = _L0_cond2_setup()
    _L0_cond2_in = {k: v for k, v in _L0_cond2_all.items() if k in ('W_sess', 'b_sess', 'W2', 'b2')}
    del _L0_cond2_all

    def _L0_ffn_setup():
        import jax, jax.numpy as jnp
        import numpy as np

        def sparsemax(z):
            E = z.shape[-1]
            z_sorted = -jnp.sort(-z, axis=-1)
            z_cum = jnp.cumsum(z_sorted, axis=-1)
            k = jnp.arange(1, E + 1, dtype=z.dtype)
            support = 1.0 + k * z_sorted > z_cum
            k_z = jnp.sum(support, axis=-1, keepdims=True)
            tau_sum = jnp.take_along_axis(z_cum, k_z.astype(jnp.int32) - 1, axis=-1)
            tau = (tau_sum - 1.0) / k_z.astype(z.dtype)
            return jnp.maximum(z - tau, 0.0)
        key = jax.random.key(seed)
        ks = jax.random.split(key, 6)
        B, S, D_IN, D_OUT, E, R = (8, 256, 512, 512, 8, 16)
        x = jax.random.normal(ks[0], (B, S, D_IN), dtype=jnp.float32)
        W_base = jax.random.normal(ks[1], (D_OUT, D_IN), dtype=jnp.float32) * D_IN ** (-0.5)
        b_base = jax.random.normal(ks[2], (D_OUT,), dtype=jnp.float32) * 0.01
        W_router = jax.random.normal(ks[3], (E, D_IN), dtype=jnp.float32) * D_IN ** (-0.5)
        b_router = jnp.zeros((E,), dtype=jnp.float32)
        lora_A = jax.random.normal(ks[4], (E, D_IN, R), dtype=jnp.float32) * D_IN ** (-0.5)
        lora_B = jnp.zeros((E, R, D_OUT), dtype=jnp.float32)
        return {'x': x, 'W_base': W_base, 'b_base': b_base, 'W_router': W_router, 'b_router': b_router, 'lora_A': lora_A, 'lora_B': lora_B}
    _L0_ffn_all = _L0_ffn_setup()
    _L0_ffn_in = {k: v for k, v in _L0_ffn_all.items() if k in ('W_base', 'b_base', 'W_router', 'b_router', 'lora_A', 'lora_B')}
    del _L0_ffn_all
    return {'x': x, 'itok_B_78_3631': itok_B_78_3631, 'itok_B_0_7': itok_B_0_7, 'itok_B_2182_4065': itok_B_2182_4065, '_lenS': _lenS, 'L0_cond_log_dt': _L0_cond_in['log_dt'], 'L0_cond_C': _L0_cond_in['C'], 'L0_cond_log_A_real': _L0_cond_in['log_A_real'], 'L0_cond_A_imag': _L0_cond_in['A_imag'], 'L0_cond_D': _L0_cond_in['D'], 'L0_attn_Wq': _L0_attn_in['Wq'], 'L0_attn_bq': _L0_attn_in['bq'], 'L0_attn_Wk': _L0_attn_in['Wk'], 'L0_attn_bk': _L0_attn_in['bk'], 'L0_attn_Wv': _L0_attn_in['Wv'], 'L0_attn_bv': _L0_attn_in['bv'], 'L0_cond2_W_sess': _L0_cond2_in['W_sess'], 'L0_cond2_b_sess': _L0_cond2_in['b_sess'], 'L0_cond2_W2': _L0_cond2_in['W2'], 'L0_cond2_b2': _L0_cond2_in['b2'], 'L0_ffn_W_base': _L0_ffn_in['W_base'], 'L0_ffn_b_base': _L0_ffn_in['b_base'], 'L0_ffn_W_router': _L0_ffn_in['W_router'], 'L0_ffn_b_router': _L0_ffn_in['b_router'], 'L0_ffn_lora_A': _L0_ffn_in['lora_A'], 'L0_ffn_lora_B': _L0_ffn_in['lora_B']}

def reference(x, itok_B_78_3631, itok_B_0_7, itok_B_2182_4065, _lenS, L0_cond_log_dt, L0_cond_C, L0_cond_log_A_real, L0_cond_A_imag, L0_cond_D, L0_attn_Wq, L0_attn_bq, L0_attn_Wk, L0_attn_bk, L0_attn_Wv, L0_attn_bv, L0_cond2_W_sess, L0_cond2_b_sess, L0_cond2_W2, L0_cond2_b2, L0_ffn_W_base, L0_ffn_b_base, L0_ffn_W_router, L0_ffn_b_router, L0_ffn_lora_A, L0_ffn_lora_B):
    import jax
    import jax.numpy as jnp

    def _L0_cond_ref(u, log_dt, C, log_A_real, A_imag, D, length):
        import math
        import jax, jax.numpy as jnp
        import numpy as np
        B, H, N, L = (16, 32, 64, 512)
        DT_MIN, DT_MAX = (0.001, 0.1)

        def _get_kernel(log_dt, C, log_A_real, A_imag, length):
            dt = jnp.exp(log_dt)
            Cc = C[..., 0] + 1j * C[..., 1]
            A = -jnp.exp(log_A_real) + 1j * A_imag
            dtA = A * dt[:, None]
            Ct = Cc * (jnp.exp(dtA) - 1.0) / A
            P = dtA[:, :, None] * jnp.arange(length, dtype=jnp.float32)
            K = 2.0 * jnp.einsum('hn,hnl->hl', Ct, jnp.exp(P)).real
            return K
        Bq, Hq, Lq = u.shape
        K = _get_kernel(log_dt, C, log_A_real, A_imag, Lq)
        n = 2 * Lq
        kf = jnp.fft.rfft(K, n=n)
        uf = jnp.fft.rfft(u, n=n)
        y = jnp.fft.irfft(uf * kf[None], n=n)[..., :Lq]
        y = y + u * D[:, None]
        mask = (jnp.arange(Lq)[None, :] < length[:, None]).astype(u.dtype)
        return y * mask[:, None, :]

    def _L0_attn_ref(x, Wq, bq, Wk, bk, Wv, bv):
        import jax, jax.numpy as jnp
        import numpy as np
        N_HEADS = 32
        N_KV_HEADS = 16
        N_EMBD = 512
        HEAD_DIM = N_EMBD // N_HEADS
        GROUPS = N_HEADS // N_KV_HEADS
        KV_DIM = N_KV_HEADS * HEAD_DIM
        SCALE = 1.0 / np.sqrt(np.float32(N_HEADS))
        B, T, C = x.shape
        q = (x @ Wq.T + bq).reshape(B, T, N_HEADS, HEAD_DIM)
        k = (x @ Wk.T + bk).reshape(B, T, N_KV_HEADS, HEAD_DIM)
        v = (x @ Wv.T + bv).reshape(B, T, N_KV_HEADS, HEAD_DIM)
        q = q.transpose(0, 2, 1, 3).reshape(B, GROUPS, N_KV_HEADS, T, HEAD_DIM)
        k = k.transpose(0, 2, 1, 3)
        v = v.transpose(0, 2, 1, 3)
        scores = jnp.einsum('bgkqd,bkld->bgkql', q, k) * SCALE
        causal = jnp.tril(jnp.ones((T, T), dtype=bool))
        scores = jnp.where(causal, scores, jnp.float32(-jnp.inf))
        w = jax.nn.softmax(scores, axis=-1)
        out = jnp.einsum('bgkql,bkld->bgkqd', w, v)
        out = out.reshape(B, N_HEADS, T, HEAD_DIM).transpose(0, 2, 1, 3).reshape(B, T, C)
        return out

    def _L0_cond2_ref(x, session_ids, channel_counts, seq_lens, W_sess, b_sess, W2, b2):
        import jax, jax.numpy as jnp
        import numpy as np
        SESSION_CHANNELS = [128, 160, 192, 224, 240, 248, 252, 32]
        N_SESS = len(SESSION_CHANNELS)
        B, MAX_C, MAX_T = (16, 32, 512)
        HID, N_SRC = (64, 32)
        cmask = (jnp.arange(x.shape[1])[None, :] < channel_counts[:, None]).astype(x.dtype)
        xm = x * cmask[:, :, None]
        W = W_sess[session_ids]
        b = b_sess[session_ids]
        h = jnp.einsum('bct,bch->bht', xm, W) + b[:, :, None]
        h = jax.nn.gelu(h, approximate=False)
        out = jnp.einsum('bht,hs->bst', h, W2) + b2[None, :, None]
        tmask = (jnp.arange(x.shape[2])[None, :] < seq_lens[:, None]).astype(x.dtype)
        return out * tmask[:, None, :]

    def _L0_ffn_ref(x, W_base, b_base, W_router, b_router, lora_A, lora_B):
        import jax, jax.numpy as jnp
        import numpy as np

        def sparsemax(z):
            E = z.shape[-1]
            z_sorted = -jnp.sort(-z, axis=-1)
            z_cum = jnp.cumsum(z_sorted, axis=-1)
            k = jnp.arange(1, E + 1, dtype=z.dtype)
            support = 1.0 + k * z_sorted > z_cum
            k_z = jnp.sum(support, axis=-1, keepdims=True)
            tau_sum = jnp.take_along_axis(z_cum, k_z.astype(jnp.int32) - 1, axis=-1)
            tau = (tau_sum - 1.0) / k_z.astype(z.dtype)
            return jnp.maximum(z - tau, 0.0)
        base_out = jnp.einsum('bsd,od->bso', x, W_base) + b_base
        logits = jnp.einsum('bsd,ed->bse', x, W_router) + b_router
        weights = sparsemax(logits)
        h = jnp.einsum('bsd,edr->bser', x, lora_A)
        expert_out = jnp.einsum('bser,bse,ero->bso', h, weights, lora_B)
        return base_out + expert_out
    x = x + _L0_attn_ref(_L0_cond_ref(x, L0_cond_log_dt, L0_cond_C, L0_cond_log_A_real, L0_cond_A_imag, L0_cond_D, itok_B_78_3631), L0_attn_Wq, L0_attn_bq, L0_attn_Wk, L0_attn_bk, L0_attn_Wv, L0_attn_bv)
    x = x + _L0_ffn_ref(_L0_cond2_ref(x, itok_B_0_7, _lenS, itok_B_2182_4065, L0_cond2_W_sess, L0_cond2_b_sess, L0_cond2_W2, L0_cond2_b2), L0_ffn_W_base, L0_ffn_b_base, L0_ffn_W_router, L0_ffn_b_router, L0_ffn_lora_A, L0_ffn_lora_B)
    return x

_drawn_inputs = setup_inputs


def setup_inputs(seed=0):
    import zlib

    import numpy as np

    out = dict(_drawn_inputs(seed))
    spreads = {'L0_cond_log_A_real': (-0.6931471824645996, 0.2),
     'L0_attn_bq': (0.0, 0.1),
     'L0_attn_bk': (0.0, 0.8),
     'L0_attn_bv': (0.0, 0.1),
     'L0_ffn_b_router': (0.0, 0.8),
     'L0_ffn_lora_B': (0.0, 0.1)}
    factors = {'L0_ffn_b_base': 7.341}
    for name, (base, spread) in spreads.items():
        noise = np.random.default_rng([zlib.crc32(name.encode()), seed]).standard_normal(out[name].shape)
        drawn = base * np.exp(spread * noise) if base else spread * noise
        out[name] = jnp.asarray(drawn.astype(out[name].dtype))
    for name, factor in factors.items():
        out[name] = (out[name] * factor).astype(out[name].dtype)
    return out
```

```python
from contextlib import ExitStack

import numpy as np
import concourse.bass as bass
from concourse import mybir

F32 = mybir.dt.float32
I32 = mybir.dt.int32
ALU = mybir.AluOpType
ACT = mybir.ActivationFunctionType
AX = mybir.AxisListType.X

B, T, C = 128, 32, 512
LB = C // 128
NG = 8
GB = B // NG
NU = GB // 4
TOK = GB * T
NMODE = 64
NSESS, HID = 8, 64
NEXP, RANK = 8, 16
KI, KK = 32, 16
PADW = 640
VW = 17
SCALE = float(1.0 / np.sqrt(np.float32(32)))
MAGIC = 12582912.0
LOG2E = 1.4426950408889634
LN2_HI, LN2_LO = 0.693359375, -2.12194440e-4
INV2PI = 0.15915494309189535
TP1, TP2 = 6.28125, 0.00193500518798828125
TP3 = 6.283185307179586 - TP1 - TP2
PI_LO = 3.1415925

PCOL, CCOL, ICOL = {}, {}, {}


def _cols(table, spec):
    at = 0
    for name, n in spec:
        table[name] = (at, at + n)
        at += n
    return at


PW = _cols(PCOL, [("logs", 64), ("aimag", 32), ("cre", 32), ("cim", 32), ("dskip", 32), ("bq", 4), ("bk", 2),
                  ("bsess", NSESS), ("b2", 1), ("brout", NEXP), ("bv", 256), ("bbase", C)])
CW = _cols(CCOL, [("turn", 3), ("angle", 3), ("lpos", LB), ("cpos", 1), ("evenodd", 2), ("own", 4),
                  ("kvec", KK), ("ivec", KI), ("causal", T), ("tpos", C), ("ident", 128)])
IW = _cols(ICOL, [("length", B), ("sid_bc", 32), ("chans", 32), ("seq", 32), ("sid_ph", 64)])


def wait(eng, sem, value):
    if isinstance(value, int) and value <= 0:
        return
    eng.wait_ge(sem, value)


def adaln_attn_ffn(nc, xT, xN, pk, cst, ints, wq, wk, wv, wsess, w2, wbase, wsmall, lorab, out, kpad, yspill):
    with ExitStack() as ctx:
        def sb(name, shape, dt=F32):
            return ctx.enter_context(nc.sbuf_tensor(name, shape, dt))

        def sem(name):
            return ctx.enter_context(nc.semaphore(name))

        P_ = sb("params", [128, PW])
        K_ = sb("consts", [128, CW])
        If = sb("ints_f", [128, IW])
        wq_s = sb("wq_s", [128, LB, C])
        wk_s = sb("wk_s", [128, LB, 256])
        wv_s = sb("wv_s", [128, LB, 256])
        wbase_s = sb("wbase_s", [128, LB, C])
        wsmall_s = sb("wsmall_s", [128, LB, 136])
        lorab_s = sb("lorab_s", [128, C])
        wsel = sb("wsel", [128, NG * NU, HID])
        w2bd = sb("w2bd", [128, 64])
        bsel = sb("bsel", [128, 64])
        wbd = sb("wbd", [128, NU, 256])
        bsg = sb("bsg", [128, 8])
        seqg = sb("seqg", [128, NU])
        ybuf = sb("ybuf", [128, LB, TOK])
        q_st = sb("q_st", [128, 4, TOK])
        k_st = sb("k_st", [128, 2, TOK])
        v_st = sb("v_st", [128, NU, 2, 8 * VW])
        kbd = sb("kbd", [128, 2, 4, TOK])
        vbd = sb("vbd", [128, NU, 4, 4, 8 * VW])
        hsm = sb("hsm", [128, NU, 136])
        c2s = sb("c2s", [128, 2, C])
        c2m = sb("c2m", [128, 2, C])
        rinv = sb("rinv", [128, 2, 16])
        rmax = sb("rmax", [128, 2, 32])
        hwT = sb("hwT", [128, NU, 128])
        ost = sb("ost", [128, 2, C])
        rt = sb("rt", [128, 8, NU * NEXP])
        pair = sb("pair", [128, 2, NU * 64])
        big = sb("big", [128, 16384])
        yT = big[:, :].rearrange("p (l b h) -> p l b h", l=LB, b=B)
        yG = big[:, :].rearrange("p (l g t) -> p l g t", l=LB, g=NG)
        S = big[:, 0:2048].rearrange("p (s n) -> p s n", s=2)
        ET = big[:, 2048:4096].rearrange("p (s n) -> p s n", s=2)
        x1 = big[:, 4096:6144].rearrange("p (u n) -> p u n", u=NU)
        xg = big[:, 6144:8192].rearrange("p (u n) -> p u n", u=NU)
        qbd = big[:, 8192:12288].rearrange("p (f b q t) -> p f b q t", f=2, b=GB, q=4)
        c2T = big[:, 12288:14336].rearrange("p (u c n) -> p u c n", u=NU, c=LB)
        gel = big[:, 14336:16384].rearrange("p (s q n) -> p s q n", s=2, q=2)
        modes = kbd[:, :, :, :].rearrange("p a b c -> p (a b c)")
        ang = vbd[:, :, :, :, :].rearrange("p a b c d -> p (a b c d)")
        wall_s = ang[:, 7968:8480].rearrange("p (s n) -> p s n", s=NSESS)
        hflat = hsm[:, :, :].rearrange("p u n -> p (u n)")
        ohs = hflat[:, 0:256].rearrange("p (s u) -> p s u", s=NSESS)
        I_ = hflat[:, 256:256 + IW].bitcast(I32)
        toep = [modes[:, C * k:C * k + C] for k in range(4)]
        xs = [ybuf[:, k, :] for k in range(4)]
        lmask = wbd[:, 0:2, :].rearrange("p u n -> p (u n)").rearrange("p (l b) -> p l b", l=LB)
        hw = c2s[:, 0, :].rearrange("p (u n) -> p u n", u=NU)

        ps = [ctx.enter_context(nc.psum_tensor(f"ps{i}", [128, 512], F32)) for i in range(8)]

        def par(name, lo=0, hi=128):
            a, b = PCOL[name]
            return P_[lo:hi, a:b]

        def con(name, lo=0, hi=128):
            a, b = CCOL[name]
            return K_[lo:hi, a:b]

        def num(name):
            a, b = ICOL[name]
            return If[:, a:b]

        names = """params_in ints_in wsess_in w2_in weights_in setup dve_step w2_zero pool_step wsel_made
            modes_made angles_made sines_made modes_ready kern_done kern_sb kpad_in
            conv_done conv_taken y_spilled y_in proj_done qk_taken v_taken qbd_made kbd_in vbd_in preset
            scores_done scores_taken row_max shifted exp_done transposed attn_done rsum_inv norm_taken
            x_in x1_made xb_made wbd_made h_done gelu_done c2_done c2_taken masked tr_done tr_taken
            small_done small_taken row_zt router_step hw_made hwT_done hwT_taken out_done out_taken""".split()
        s = {n: sem(n) for n in names}
        (params_in, ints_in, wsess_in, w2_in, weights_in, setup, dve_step, w2_zero, pool_step, wsel_made,
         modes_made, angles_made, sines_made, modes_ready, kern_done, kern_sb, kpad_in,
         conv_done, conv_taken, y_spilled, y_in, proj_done, qk_taken, v_taken, qbd_made, kbd_in, vbd_in, preset,
         scores_done, scores_taken, row_max, shifted, exp_done, transposed, attn_done, rsum_inv, norm_taken,
         x_in, x1_made, xb_made, wbd_made, h_done, gelu_done, c2_done, c2_taken, masked, tr_done, tr_taken,
         small_done, small_taken, row_zt, router_step, hw_made, hwT_done, hwT_taken, out_done, out_taken) = [s[n] for n in names]
        toep_in = [sem(f"toep_in{k}") for k in range(4)]
        xs_in = [sem(f"xs_in{k}") for k in range(4)]
        stored = [sem(f"stored{k}") for k in range(2)]

        NV, NUU = 32 * KK, 32 * KI
        th = modes[:, 0:96]
        thV = modes[:, 96:96 + NV]
        thU = modes[:, 608:608 + NUU]
        red = ang[:, 0:2656]
        tmpa = ang[:, 2656:5312]
        snb = ang[:, 5312:7968]
        expV = modes[:, 1632:2144]
        expU = modes[:, 2144:3168]
        L_ = q_st[:, 0:2, :].rearrange("p a b -> p (a b)")
        R_ = q_st[:, 2, :]
        tU = modes[:, 3168:4096]
        ksb = k_st[0:32, 0, :]
        zrow = k_st[0:32, 1, 0:128]

        def small(n):
            return tU[:, 32 * n:32 * n + 32]

        def small2(n):
            return tU[:, 32 * n:32 * n + 64]

        block = ctx.enter_context(nc.Block())

        @block.sync
        def _(sp):
            sp.dma_start(P_[:, :], pk).then_inc(params_in, 16)
            sp.dma_start(K_[:, :], cst).then_inc(params_in, 16)
            sp.dma_start(I_[:, :], ints).then_inc(ints_in, 16)

            def load_x(t, k):
                if not isinstance(t, int) or t > 0:
                    sp.wait_ge(conv_done, 4 * t + k - 3)
                    sp.wait_ge(ints_in, 16)
                sp.dma_start(xs[k], xT[4 * t + k]).then_inc(xs_in[k], 16)

            for k in range(4):
                load_x(0, k)
            sp.dma_start(wq_s[:, :, :], wq).then_inc(weights_in, 16)
            sp.dma_start(wk_s[:, :, :], wk).then_inc(weights_in, 16)
            sp.dma_start(wv_s[:, :, :], wv).then_inc(weights_in, 16)
            sp.dma_start(wbase_s[:, :, :], wbase).then_inc(weights_in, 16)
            sp.dma_start(wsmall_s[:, :, :], wsmall).then_inc(weights_in, 16)
            sp.dma_start(lorab_s[:, :], lorab).then_inc(weights_in, 16)
            with sp.Fori(1, 8) as t:
                for k in range(4):
                    load_x(t, k)
            sp.wait_ge(conv_taken, 32)
            sp.dma_start(ybuf[:, :, :], yG[:, :, 0, :]).then_inc(y_in, 16)
            for g in range(1, NG):
                sp.dma_start(yspill[g], yG[:, :, g, :]).then_inc(y_spilled, 16)

            def place_k(j, waits):
                if waits:
                    wait(sp, scores_done, 8 * j)
                wait(sp, qk_taken, 6 * j + 6)
                for e in range(2):
                    for r in range(4):
                        p = 64 * e + 16 * r
                        sp.dma_start(kbd[p:p + 16, :, r, :], k_st[p:p + 16, :, :]).then_inc(kbd_in, 16)

            def place_v(j, waits):
                wait(sp, v_taken, 4 * j + 4)
                if waits:
                    wait(sp, attn_done, 8 * j)
                for b in range(4):
                    for ge in range(4):
                        sp.dma_start(vbd[32 * ge:32 * ge + 32, :, b, ge, :],
                                     v_st[32 * b:32 * b + 32, :, ge % 2, :]).then_inc(vbd_in, 16)

            def load_y(j):
                wait(sp, proj_done, 10 * j)
                sp.wait_ge(y_spilled, 16 * (NG - 1))
                sp.dma_start(ybuf[:, :, :], yspill[j]).then_inc(y_in, 16)

            sp.wait_ge(preset, 3)
            place_k(0, False)
            place_v(0, False)
            load_y(1)
            for u in range(NU):
                sp.dma_start(xg[:, u, :], xN[0, :, u, :]).then_inc(x_in, 16)

            def group(i, more_y, more):
                if more:
                    place_k(i + 1, True)
                    place_v(i + 1, True)
                if more_y:
                    load_y(i + 2)
                for u in range(NU):
                    sp.wait_ge(out_taken, 4 * i + u + 1)
                    sp.wait_ge(ints_in, 16)
                    sp.dma_start(out[i, :, u, :], ost[:, u % 2, :]).then_inc(stored[u % 2], 16)
                    if more:
                        sp.dma_start(xg[:, u, :], xN[i + 1, :, u, :]).then_inc(x_in, 16)

            group(0, True, True)
            with sp.Fori(1, 6) as i:
                group(i, True, True)
            group(6, False, True)
            group(7, False, False)
            sp.wait_ge(stored[0], 16 * 2 * NG)
            sp.wait_ge(stored[1], 16 * 2 * NG)

        @block.tensor
        def _(pe):
            pe.wait_ge(modes_ready, 1)
            for h in range(32):
                mm = pe.matmul(ps[7][0:32, h * KK:(h + 1) * KK], L_[:, h * KI:(h + 1) * KI],
                               R_[:, h * KK:(h + 1) * KK], start=True, stop=True)
            mm.then_inc(kern_done, 1)

            def conv(t, k):
                pe.wait_ge(toep_in[k], 16 * t + 16)
                pe.wait_ge(xs_in[k], 16 * t + 16)
                if not isinstance(t, int) or t > 0:
                    pe.wait_ge(conv_taken, 4 * t + k - 3)
                for d in range(LB):
                    mm = pe.matmul(ps[k][:, 128 * d:512], toep[k][:, 128 * d:128 * d + 128],
                                   xs[k][:, 0:512 - 128 * d], start=(d == 0), stop=(d == LB - 1))
                mm.then_inc(conv_done, 1)

            for k in range(4):
                conv(0, k)
            with pe.Fori(1, 8) as t:
                for k in range(4):
                    conv(t, k)

            def project(j, c):
                bank = ps[4 + c % 2]
                if c == 0:
                    pe.wait_ge(y_in, 16 * j + 16)
                    wait(pe, small_taken, 4 * (j - 1))
                elif 2 <= c <= 7:
                    pe.wait_ge(qk_taken, 6 * j + c - 1)
                elif c >= 8:
                    pe.wait_ge(v_taken, 4 * j + c - 7)
                for l in range(LB):
                    f = dict(start=(l == 0), stop=(l == LB - 1))
                    if c < 4:
                        mm = pe.matmul(bank[:, :], wq_s[:, l, 128 * c:128 * c + 128], ybuf[:, l, :], **f)
                    elif c < 6:
                        mm = pe.matmul(bank[:, :], wk_s[:, l, 128 * (c - 4):128 * (c - 3)], ybuf[:, l, :], **f)
                    else:
                        u = c - 6
                        mm = pe.matmul(bank[:, 0:256], ybuf[:, l, 128 * u:128 * u + 128], wv_s[:, l, :], **f)
                mm.then_inc(proj_done, 1)

            def scores(i, u):
                n = 4 * i + u
                if u == 0:
                    pe.wait_ge(qbd_made, 8 * i + 8)
                    pe.wait_ge(kbd_in, 16 * 8 * (i + 1))
                    wait(pe, hwT_taken, i)
                    wait(pe, tr_taken, 4 * i)
                for k in range(2):
                    wait(pe, scores_taken, 2 * n + k - 1)
                    for b in (4 * u + 2 * k, 4 * u + 2 * k + 1):
                        for f in range(2):
                            at = 256 * (b % 2) + 128 * f
                            mm = pe.matmul(ps[k][:, at:at + 128], qbd[:, f, b, :, :],
                                           kbd[:, f, :, 32 * b:32 * b + 32], start=True, stop=True)
                    mm.then_inc(scores_done, 1)

            def attend(i, u):
                n = 4 * i + u
                if u == 0:
                    pe.wait_ge(vbd_in, 16 * 16 * (i + 1))
                    wait(pe, out_taken, 4 * i)
                pe.wait_ge(transposed, n + 1)
                for f in range(2):
                    wait(pe, norm_taken, 2 * n + f - 1)
                    for b in range(4):
                        for r in range(4):
                            at = 256 * b + 128 * f + 32 * r
                            v = (4 * f + r) * VW
                            mm = pe.matmul(ps[2 + f][32 * b:32 * b + 32, 68 * r:68 * r + 68],
                                           ET[:, u % 2, at:at + 32], vbd[:, u, b, :, v:v + VW],
                                           start=True, stop=True)
                    mm.then_inc(attn_done, 1)

            def cond_h(i, u):
                n = 4 * i + u
                pe.wait_ge(x1_made, n + 1)
                if u == 0:
                    pe.wait_ge(wbd_made, 6 * i + 6)
                for p in range(2):
                    wait(pe, gelu_done, 2 * n + p - 1)
                    pe.matmul(ps[6 + p][:, :], wbd[:, u, 128 * p:128 * p + 128], x1[:, u, :],
                              start=True, stop=True).then_inc(h_done, 1)

            def cond_out(i, u):
                n = 4 * i + u
                pe.wait_ge(gelu_done, 2 * n + 2)
                if u == 0:
                    pe.wait_ge(scores_taken, 8 * i + 8)
                wait(pe, c2_taken, n)
                for p in range(2):
                    mm = pe.matmul(ps[0][64 * p:64 * p + 64, :], w2bd[:, :], gel[:, u % 2, p, :],
                                   start=True, stop=True)
                mm.then_inc(c2_done, 1)

            def turn(i, u):
                n = 4 * i + u
                pe.wait_ge(masked, n + 1)
                wait(pe, tr_taken, n)
                for c in range(LB):
                    mm = pe.transpose(ps[1][:, 128 * c:128 * c + 128], c2m[:, u % 2, 128 * c:128 * c + 128],
                                      con("ident"))
                mm.then_inc(tr_done, 1)

            def router_lora(i, u, last):
                n = 4 * i + u
                pe.wait_ge(tr_taken, n + 1)
                if u < 2:
                    pe.wait_ge(v_taken, 4 * i + (4 if last else 8))
                else:
                    pe.wait_ge(small_taken, n - 1)
                for c in range(LB):
                    mm = pe.matmul(ps[4 + u % 2][:, 0:136], c2T[:, u, c, :], wsmall_s[:, c, :],
                                   start=(c == 0), stop=(c == LB - 1))
                mm.then_inc(small_done, 1)

            out_bank = [ps[2], ps[3], ps[6], ps[7]]

            def base(i, u):
                if u == 0:
                    pe.wait_ge(norm_taken, 8 * i + 8)
                if u == 2:
                    pe.wait_ge(gelu_done, 8 * i + 8)
                for c in range(LB):
                    pe.matmul(out_bank[u][:, :], c2T[:, u, c, :], wbase_s[:, c, :], start=(c == 0), stop=False)

            def turn_h(i):
                pe.wait_ge(hw_made, i + 1)
                pe.wait_ge(c2_taken, 4 * i + 4)
                for u in range(NU):
                    mm = pe.transpose(ps[0][:, 128 * u:128 * u + 128], hw[:, u, :], con("ident"))
                mm.then_inc(hwT_done, 1)

            def expert(i, u):
                if u == 0:
                    pe.wait_ge(hwT_taken, i + 1)
                pe.matmul(out_bank[u][:, :], hwT[:, u, :], lorab_s[:, :], start=False, stop=True).then_inc(out_done, 1)

            def group(i, last=False):
                def A(c):
                    if not last:
                        project(i + 1, c)
                scores(i, 0); A(0)
                scores(i, 1); A(1); attend(i, 0); A(2)
                scores(i, 2); A(3); attend(i, 1); A(4)
                scores(i, 3); A(5); attend(i, 2); A(6)
                attend(i, 3); A(7); A(8); A(9)
                for k in range(NU + 3):
                    if k < NU:
                        cond_h(i, k)
                    if 1 <= k <= NU:
                        cond_out(i, k - 1)
                    if 2 <= k <= NU + 1:
                        turn(i, k - 2)
                    if k >= 3:
                        router_lora(i, k - 3, last)
                base(i, 0); base(i, 1)
                turn_h(i)
                base(i, 2)
                expert(i, 0); expert(i, 1); expert(i, 2)
                base(i, 3)
                expert(i, 3)

            pe.wait_ge(weights_in, 16 * 6)
            for c in range(10):
                project(0, c)
            pe.wait_ge(w2_in, 32)
            group(0)
            with pe.Fori(1, 7) as i:
                group(i)
            group(7, last=True)

        @block.scalar
        def _(act):
            for q in range(4):
                act.dma_start(wall_s[32 * q:32 * q + 32, :, :], wsess).then_inc(wsess_in, 16)
            act.wait_ge(w2_zero, 1)
            for p in range(2):
                act.dma_start(w2bd[64 * p:64 * p + 64, 32 * p:32 * p + 32], w2).then_inc(w2_in, 16)
            act.wait_ge(modes_made, 1)
            act.activation(small(6), small(5), ACT.Tanh, scale=0.5).then_inc(sines_made, 1)
            act.activation(expV, expV, ACT.Exp).then_inc(sines_made, 1)
            act.activation(expU, expU, ACT.Exp).then_inc(sines_made, 1)
            act.wait_ge(angles_made, 1)
            act.activation(snb, red, ACT.Sin).then_inc(sines_made, 1)
            act.wait_ge(kern_sb, 2)
            act.dma_start(kpad[:, 0:127], zrow[:, 0:127]).then_inc(kpad_in, 16)
            act.dma_start(kpad[:, 127:127 + C].rearrange("h (i k) -> i h k", k=KK),
                          ksb.rearrange("i (h k) -> i h k", k=KK)).then_inc(kpad_in, 16)
            act.wait_ge(kpad_in, 32)

            def load_toep(t, k):
                if not isinstance(t, int) or t > 0:
                    act.wait_ge(conv_done, 4 * t + k - 3)
                    act.wait_ge(kpad_in, 32)
                rows = bass.AP(kpad.tensor, (4 * t + k) * PADW + kpad.offset, [[1, 128], [1, C]])
                act.dma_start(toep[k], rows).then_inc(toep_in[k], 16)

            for k in range(4):
                load_toep(0, k)
            with act.Fori(1, 8) as t:
                for k in range(4):
                    load_toep(t, k)

            def take(j, c):
                act.wait_ge(proj_done, 10 * j + c + 1)
                if c == 0:
                    wait(act, qbd_made, 8 * j)
                if c == 4:
                    wait(act, kbd_in, 16 * 8 * j)
                if c < 4:
                    act.activation(q_st[:, c, :], ps[4 + c % 2][:, :], ACT.Identity,
                                   bias=par("bq")[:, c:c + 1]).then_inc(qk_taken, 1)
                else:
                    act.activation(k_st[:, c - 4, :], ps[4 + c % 2][:, :], ACT.Identity,
                                   bias=par("bk")[:, c - 4:c - 3]).then_inc(qk_taken, 1)

            def expo(i, u):
                act.wait_ge(shifted, 4 * i + u + 1)
                act.activation(S[:, u % 2, :], S[:, u % 2, :], ACT.Exp, scale=SCALE).then_inc(exp_done, 1)

            def gelu(i, u, p):
                n = 4 * i + u
                act.wait_ge(h_done, 2 * n + p + 1)
                wait(act, c2_done, n - 1)
                act.activation(gel[:, u % 2, p, :], ps[6 + p][:, :], ACT.Gelu,
                               bias=bsg[:, 2 * u + p:2 * u + p + 1]).then_inc(gelu_done, 1)

            def take_c2(i, u):
                n = 4 * i + u
                act.wait_ge(c2_done, n + 1)
                wait(act, masked, n - 1)
                act.activation(c2s[:, u % 2, :], ps[0][:, :], ACT.Identity, bias=par("b2")).then_inc(c2_taken, 1)

            def take_turned(i, u):
                act.wait_ge(tr_done, 4 * i + u + 1)
                wait(act, out_done, 4 * i)
                act.activation(c2T[:, u, :, :], ps[1][:, :].rearrange("p (c n) -> p c n", c=LB),
                               ACT.Copy).then_inc(tr_taken, 1)

            def take_small(i, u):
                act.wait_ge(small_done, 4 * i + u + 1)
                wait(act, hw_made, i)
                act.activation(hsm[:, u, :], ps[4 + u % 2][:, 0:136], ACT.Copy).then_inc(small_taken, 1)

            def take_hw(i):
                act.wait_ge(hwT_done, i + 1)
                wait(act, out_done, 4 * i)
                act.activation(hwT[:, :, :], ps[0][:, :].rearrange("p (u n) -> p u n", u=NU),
                               ACT.Copy).then_inc(hwT_taken, 1)

            def group(i, last=False):
                def A(c):
                    if not last:
                        take(i + 1, c)
                expo(i, 0); A(0)
                expo(i, 1); A(1); A(2)
                expo(i, 2); A(3); A(4)
                expo(i, 3); A(5)
                for k in range(NU + 3):
                    if k < NU:
                        gelu(i, k, 0); gelu(i, k, 1)
                    if 1 <= k <= NU:
                        take_c2(i, k - 1)
                    if 2 <= k <= NU + 1:
                        take_turned(i, k - 2)
                    if k >= 3:
                        take_small(i, k - 3)
                take_hw(i)

            act.wait_ge(wsel_made, 1)
            for c in range(6):
                take(0, c)
            group(0)
            with act.Fori(1, 7) as i:
                group(i)
            group(7, last=True)

        @block.gpsimd
        def _(pool):
            steps = [0]

            def step(ins):
                steps[0] += 1
                ins.then_inc(pool_step, 1)
                pool.wait_ge(pool_step, steps[0])

            pool.memset(w2bd[:, :], 0.0).then_inc(w2_zero, 1)
            pool.wait_ge(wsess_in, 64)
            pool.wait_ge(setup, 8)
            pool.wait_ge(kern_done, 1)
            tmp = q_st[:, :, :].rearrange("p a b -> p (a b)").rearrange("p (u n) -> p u n", u=32)
            for k in range(NSESS):
                dst = wsel[:, :, :] if k == 0 else tmp
                step(pool.tensor_tensor(dst, wall_s[:, k:k + 1, :].broadcast_to([128, 32, HID]),
                                        ohs[:, k, :].rearrange("p (u o) -> p u o", o=1).broadcast_to([128, 32, HID]),
                                        ALU.mult))
                if k:
                    ins = pool.tensor_tensor(wsel[:, :, :], wsel[:, :, :], tmp, ALU.add)
                    if k < NSESS - 1:
                        step(ins)
                    else:
                        ins.then_inc(wsel_made, 1)
            pool.wait_ge(wsel_made, 1)
            pool.wait_ge(conv_taken, 32)
            pool.memset(kbd[:, :, :, :], 0.0).then_inc(preset, 1)
            pool.memset(vbd[:, :, :, :, :], 0.0).then_inc(preset, 1)
            pool.memset(v_st[:, :, :, :], 1.0).then_inc(preset, 1)

            def residual(i, u):
                n = 4 * i + u
                if u == 0:
                    pool.wait_ge(x_in, 64 * i + 64)
                pool.wait_ge(norm_taken, 2 * n + 2)
                pool.tensor_tensor(x1[:, u, :], x1[:, u, :], xg[:, u, :], ALU.add).then_inc(x1_made, 1)
                pool.wait_ge(x1_made, n + 1)
                pool.tensor_tensor(xg[:, u, :], x1[:, u, :], par("bbase"), ALU.add).then_inc(xb_made, 1)

            def conditions(i):
                for u in range(NU):
                    w = wsel[:, 4 * i + u, :] if isinstance(i, int) else wsel[:, bass.ds(4 * i + u, 1), :]
                    w = w.rearrange("p n -> p () n") if isinstance(i, int) else w
                    pool.tensor_tensor(wbd[:, u, :].rearrange("p (b n) -> p b n", b=4),
                                       w.broadcast_to([128, 4, HID]),
                                       con("own").rearrange("p (b o) -> p b o", o=1).broadcast_to([128, 4, HID]),
                                       ALU.mult).then_inc(wbd_made, 1)
                pool.tensor_copy(bsg[:, :], bsel[:, bass.ds(8 * i, 8)]).then_inc(wbd_made, 1)
                a = ICOL["seq"][0]
                pool.tensor_copy(seqg[:, :], If[:, bass.ds(a + 4 * i, 4)]).then_inc(wbd_made, 1)

            def group(i):
                residual(i, 0)
                conditions(i)
                for u in range(1, NU):
                    residual(i, u)

            pool.wait_ge(setup, 10)
            group(0)
            with pool.Fori(1, 8) as i:
                group(i)

        @block.vector
        def _(dve):
            steps = [0]

            def step(ins):
                steps[0] += 1
                ins.then_inc(dve_step, 1)
                dve.wait_ge(dve_step, steps[0])

            def tt(o, a, b, op):
                step(dve.tensor_tensor(o, a, b, op))

            def ts(o, a, s1, op0, s2=None, op1=None):
                if s2 is None:
                    step(dve.tensor_scalar(o, a, s1, None, op0))
                else:
                    step(dve.tensor_scalar(o, a, s1, s2, op0, op1))

            def stt(o, a, sc, b, op0, op1):
                step(dve.scalar_tensor_tensor(out=o, in0=a, scalar=sc, in1=b, op0=op0, op1=op1))

            dve.wait_ge(params_in, 32)
            dve.memset(zrow, 0.0).then_inc(kern_sb, 1)
            X, N_, R, PL = par("logs"), small2(0), small2(2), small2(8)
            ts(N_, X, LOG2E, ALU.mult, MAGIC, ALU.add)
            ts(N_, N_, MAGIC, ALU.subtract)
            stt(R, N_, -LN2_HI, X, ALU.mult, ALU.add)
            stt(R, N_, -LN2_LO, R, ALU.mult, ALU.add)
            ts(PL, R, 1.0 / 5040, ALU.mult)
            for c in (1.0 / 720, 1.0 / 120, 1.0 / 24, 1.0 / 6, 0.5, 1.0):
                stt(PL, PL, c, R, ALU.add, ALU.mult)
            ts(PL, PL, 1.0, ALU.add)
            ts(N_, N_, 127.0, ALU.add, 8388608.0, ALU.mult)
            step(dve.tensor_copy(R.bitcast(I32), N_))
            tt(PL, PL, R, ALU.mult)
            dt, am = small(8), small(9)
            dr = small(5)
            stt(dr, am, -1.0, dt, ALU.mult, ALU.mult)
            tt(th[:, 0:32], par("aimag"), dt, ALU.mult)
            ts(th[:, 32:64], th[:, 0:32], 1.0, ALU.mult)
            ts(th[:, 64:96], th[:, 0:32], 0.5, ALU.mult)

            def outer(o, a, vec, n):
                tt(o.rearrange("p (h n) -> p h n", h=32), a.rearrange("p (h o) -> p h o", o=1).broadcast_to([128, 32, n]),
                   con(vec).rearrange("p (o n) -> p o n", o=1).broadcast_to([128, 32, n]), ALU.mult)

            outer(expV, dr, "kvec", KK)
            outer(expU, dr, "ivec", KI)
            dve.tensor_copy(small(4), dr).then_inc(modes_made, 1)
            outer(thV, th[:, 0:32], "kvec", KK)
            outer(thU, th[:, 0:32], "ivec", KI)
            turn, angle = con("turn"), con("angle")
            parts = [(th[:, 0:32], 0.0, 0.0, 0, 32), (th[:, 32:64], 0.25, float(np.pi / 2), 32, 64),
                     (th[:, 64:96], 0.0, 0.0, 64, 96),
                     (thV, turn[:, 0:1], angle[:, 0:1], 96, 608), (thU, turn[:, 1:2], angle[:, 1:2], 608, 1632),
                     (thU, turn[:, 2:3], angle[:, 2:3], 1632, 2656)]
            for a, q, _w, lo, hi in parts:
                ts(tmpa[:, lo:hi], a, INV2PI, ALU.mult, q, ALU.add)
            ts(tmpa, tmpa, MAGIC, ALU.add)
            ts(tmpa, tmpa, MAGIC, ALU.subtract)
            for a, _q, w, lo, hi in parts:
                stt(red[:, lo:hi], tmpa[:, lo:hi], -TP1, a, ALU.mult, ALU.add)
            stt(red, tmpa, -TP2, red, ALU.mult, ALU.add)
            stt(red, tmpa, -TP3, red, ALU.mult, ALU.add)
            for a, _q, w, lo, hi in parts[1:]:
                ts(red[:, lo:hi], red[:, lo:hi], w, ALU.add)
            steps[0] += 1
            dve.tensor_scalar(red, red, PI_LO, -PI_LO, ALU.min, ALU.max).then_inc(dve_step, 1)
            dve.wait_ge(dve_step, steps[0])
            dve.tensor_copy(small(7)[:, 0:1], small(4)[:, 0:1]).then_inc(angles_made, 1)
            dve.wait_ge(sines_made, 4)
            tn, em, er, ei = small(6), small(0), small(1), small(2)
            sn, cs, sh = snb[:, 0:32], snb[:, 32:64], snb[:, 64:96]
            ts(er, tn, -1.0, ALU.mult, 1.0, ALU.add)
            step(dve.reciprocal(er, er))
            stt(em, tn, 2.0, er, ALU.mult, ALU.mult)
            stt(ei, em, 1.0, sn, ALU.add, ALU.mult)
            tt(er, em, cs, ALU.mult)
            tt(em, sh, sh, ALU.mult)
            stt(er, em, -2.0, er, ALU.mult, ALU.add)
            ai, den, t0, t1 = par("aimag"), small(3), small(7), small(10)
            nr, ni = small(11), small(12)
            tt(t0, am, am, ALU.mult)
            tt(den, ai, ai, ALU.mult)
            tt(den, den, t0, ALU.add)
            step(dve.reciprocal(den, den))
            cre, cim = par("cre"), par("cim")
            tt(nr, cre, er, ALU.mult)
            tt(t0, cim, ei, ALU.mult)
            tt(nr, nr, t0, ALU.subtract)
            tt(ni, cre, ei, ALU.mult)
            tt(t0, cim, er, ALU.mult)
            tt(ni, ni, t0, ALU.add)
            tt(t0, nr, am, ALU.mult)
            tt(t1, ni, ai, ALU.mult)
            tt(t0, t1, t0, ALU.subtract)
            tt(t1, nr, ai, ALU.mult)
            tt(nr, ni, am, ALU.mult)
            tt(t1, t1, nr, ALU.add)
            stt(small(11), t0, 2.0, den, ALU.mult, ALU.mult)
            stt(small(12), t1, -2.0, den, ALU.mult, ALU.mult)
            cr, ci = small(11), small(12)

            def bc(a, n):
                return a.rearrange("p (h o) -> p h o", o=1).broadcast_to([128, 32, n])

            def v3(a):
                return a.rearrange("p (h n) -> p h n", h=32)

            tt(R_, expV, snb[:, 96:608], ALU.mult)
            tt(v3(L_), v3(snb[:, 608:1632]), bc(cr, KI), ALU.mult)
            tt(v3(tmpa[:, 0:1024]), v3(snb[:, 1632:2656]), bc(ci, KI), ALU.mult)
            tt(L_, L_, tmpa[:, 0:1024], ALU.add)
            dve.tensor_tensor(L_, L_, expU, ALU.mult).then_inc(modes_ready, 1)
            dve.wait_ge(kern_done, 1)
            step(dve.tensor_copy(ksb, ps[7][0:32, :]))
            k0 = ksb[0:1, :].rearrange("p (h k) -> p h k", h=32)[:, :, 0]
            dve.tensor_tensor(k0, k0, par("dskip", 0, 1), ALU.add).then_inc(kern_sb, 1)

            dve.wait_ge(ints_in, 16)
            step(dve.tensor_copy(If[:, :], I_[:, :]))
            for l in range(LB):
                ts(lmask[:, l, :], num("length"), con("lpos")[:, l:l + 1], ALU.is_gt)
            cm = rmax[:, 0, :]
            ts(cm, num("chans"), con("cpos"), ALU.is_gt)
            for k in range(NSESS):
                dve.scalar_tensor_tensor(out=ohs[:, k, :], in0=num("sid_bc"), scalar=float(k), in1=cm,
                                         op0=ALU.is_equal, op1=ALU.mult).then_inc(setup, 1)
            bs = par("bsess")
            for k in range(NSESS):
                dst = bsel[:, :] if k == 0 else pair[:, 0, 0:64]
                ts(dst, num("sid_ph"), float(k), ALU.is_equal, bs[:, k:k + 1], ALU.mult)
                if k:
                    tt(bsel[:, :], bsel[:, :], pair[:, 0, 0:64], ALU.add)
            dve.tensor_copy(pair[:, 1, 0:64], bsel[:, :]).then_inc(setup, 1)
            dve.tensor_copy(pair[:, 1, 64:96], num("seq")).then_inc(setup, 1)

            def take_conv(t, k):
                dve.wait_ge(conv_done, 4 * t + k + 1)
                h = 4 * t + k
                o = yT[:, :, :, h] if isinstance(t, int) else yT[:, :, :, bass.ds(h, 1)].rearrange("p l b o -> p l (b o)")
                dve.tensor_tensor(o, ps[k][:, :].rearrange("p (l b) -> p l b", l=LB), lmask[:, :, :],
                                  ALU.mult).then_inc(conv_taken, 1)

            for k in range(4):
                take_conv(0, k)
            with dve.Fori(1, 8) as t:
                for k in range(4):
                    take_conv(t, k)

            causal = con("causal").rearrange("p (o n) -> p o n", o=1).broadcast_to([128, 16, T])

            def take_v(j, u):
                dve.wait_ge(proj_done, 10 * j + 7 + u)
                if u == 0:
                    wait(dve, vbd_in, 16 * 16 * j)
                dve.tensor_tensor(v_st[:, u, :, :].rearrange("p e (k w) -> p (e k) w", w=VW)[:, :, 0:16],
                                  ps[4 + u % 2][:, 0:256].rearrange("p (k w) -> p k w", w=16),
                                  par("bv").rearrange("p (k w) -> p k w", w=16), ALU.add).then_inc(v_taken, 1)

            def spread_q(j, waits):
                wait(dve, qk_taken, 6 * j + 4)
                if waits:
                    wait(dve, scores_done, 8 * j)
                else:
                    dve.wait_ge(y_spilled, 16 * (NG - 1))
                    dve.wait_ge(y_in, 16)
                for g in range(2):
                    for f in range(2):
                        for e in range(2):
                            dve.tensor_scalar(qbd[:, f, :, 2 * g + e, :],
                                              q_st[:, 2 * g + f, :].rearrange("p (b t) -> p b t", b=GB),
                                              con("evenodd")[:, e:e + 1], None, ALU.mult).then_inc(qbd_made, 1)

            def soft(i, u):
                n = 4 * i + u
                Su = S[:, u % 2, :]
                for k in range(2):
                    dve.wait_ge(scores_done, 2 * n + k + 1)
                    dve.tensor_tensor(Su[:, 512 * k:512 * k + 512].rearrange("p (m n) -> p m n", n=T),
                                      ps[k][:, :].rearrange("p (m n) -> p m n", n=T), causal,
                                      ALU.add).then_inc(scores_taken, 1)
                dve.wait_ge(scores_taken, 2 * n + 2)
                S3 = Su.rearrange("p (m n) -> p m n", n=T)
                dve.tensor_reduce(rmax[:, u % 2, :], S3, AX, ALU.max).then_inc(row_max, 1)
                dve.wait_ge(row_max, n + 1)
                dve.tensor_tensor(S3, S3, rmax[:, u % 2, :].rearrange("p (m o) -> p m o", o=1).broadcast_to([128, 32, T]),
                                  ALU.subtract).then_inc(shifted, 1)

            def turn_p(i, u):
                n = 4 * i + u
                dve.wait_ge(exp_done, n + 1)
                wait(dve, attn_done, 2 * n - 2)
                dve.transpose(ET[:, u % 2, :], S[:, u % 2, :]).then_inc(transposed, 1)

            def normalise(i, u):
                n = 4 * i + u
                for f in range(2):
                    dve.wait_ge(attn_done, 2 * n + f + 1)
                    pv = ps[2 + f][:, 0:16 * VW].rearrange("p (m w) -> p m w", w=VW)
                    dve.reciprocal(rinv[:, f, :], pv[:, :, 16]).then_inc(rsum_inv, 1)
                    if f == 0:
                        wait(dve, h_done, 8 * i)
                        wait(dve, xb_made, 4 * i)
                    dve.wait_ge(rsum_inv, 2 * n + f + 1)
                    dve.tensor_tensor(x1[:, u, 256 * f:256 * f + 256].rearrange("p (m w) -> p m w", w=16),
                                      pv[:, :, 0:16],
                                      rinv[:, f, :].rearrange("p (m o) -> p m o", o=1).broadcast_to([128, 16, 16]),
                                      ALU.mult).then_inc(norm_taken, 1)

            def mask_c2(i, u):
                n = 4 * i + u
                dve.wait_ge(c2_taken, n + 1)
                wait(dve, tr_done, n - 1)
                dve.scalar_tensor_tensor(out=c2m[:, u % 2, :], in0=con("tpos"), scalar=seqg[:, u:u + 1],
                                         in1=c2s[:, u % 2, :], op0=ALU.is_lt, op1=ALU.mult).then_inc(masked, 1)

            NR = 12

            def route(i):
                k = [0]

                def r(ins):
                    k[0] += 1
                    ins.then_inc(router_step, 1)
                    dve.wait_ge(router_step, NR * i + k[0])

                def t3(x):
                    return x.rearrange("p (u e) -> p u e", u=NU)

                z, ki, ci_, su, sz = (rt[:, m, :] for m in range(5))
                kz, tau = rt[:, 5, 0:NU], rt[:, 6, 0:NU]
                G = pair[:, 0, :].rearrange("p (m j) -> p m j", j=NEXP)
                GZ = pair[:, 1, :].rearrange("p (m j) -> p m j", j=NEXP)

                def ui(x):
                    return x.rearrange("p (m o) -> p m o", o=1).broadcast_to([128, NU * NEXP, NEXP])

                def uj(x):
                    return x.rearrange("p (u o e) -> p u o e", u=NU, o=1).broadcast_to([128, NU, NEXP, NEXP])

                def u4(x):
                    return x.rearrange("p (u i) j -> p u i j", u=NU)

                dve.wait_ge(small_taken, 4 * i + 4)
                r(dve.tensor_tensor(t3(z), hsm[:, :, 0:NEXP],
                                    par("brout").rearrange("p (o e) -> p o e", o=1).broadcast_to([128, NU, NEXP]),
                                    ALU.add))
                r(dve.tensor_tensor(u4(G), uj(z), u4(ui(z)), ALU.is_ge))
                r(dve.tensor_tensor(u4(GZ), u4(G), uj(z), ALU.mult))
                r(dve.tensor_reduce(ki, G, AX, ALU.add))
                r(dve.tensor_reduce(ci_, GZ, AX, ALU.add))
                r(dve.tensor_tensor(su, z, ki, ALU.mult))
                r(dve.scalar_tensor_tensor(out=su, in0=su, scalar=1.0, in1=ci_, op0=ALU.add, op1=ALU.is_gt))
                r(dve.tensor_tensor(sz, su, z, ALU.mult))
                r(dve.tensor_reduce(kz, t3(su), AX, ALU.add))
                r(dve.tensor_reduce(tau, t3(sz), AX, ALU.add))
                r(dve.reciprocal(kz, kz))
                r(dve.scalar_tensor_tensor(out=tau, in0=tau, scalar=-1.0, in1=kz, op0=ALU.add, op1=ALU.mult))
                assert k[0] == NR

            def weigh(i):
                z, zt, tau = rt[:, 0, :], rt[:, 7, :], rt[:, 6, 0:NU]
                dve.tensor_tensor(zt.rearrange("p (u e) -> p u e", u=NU), z.rearrange("p (u e) -> p u e", u=NU),
                                  tau.rearrange("p (u o) -> p u o", o=1).broadcast_to([128, NU, NEXP]),
                                  ALU.subtract).then_inc(row_zt, 1)
                dve.wait_ge(row_zt, 2 * i + 1)
                dve.tensor_scalar(zt, zt, 0.0, None, ALU.max).then_inc(row_zt, 1)
                wait(dve, hwT_done, i)
                dve.wait_ge(row_zt, 2 * i + 2)
                dve.tensor_tensor(hw[:, :, :].rearrange("p u (e r) -> p u e r", e=NEXP),
                                  hsm[:, :, NEXP:136].rearrange("p u (e r) -> p u e r", e=NEXP),
                                  zt.rearrange("p (u e o) -> p u e o", u=NU, o=1).broadcast_to([128, NU, NEXP, RANK]),
                                  ALU.mult).then_inc(hw_made, 1)

            def final(i, u):
                n = 4 * i + u
                dve.wait_ge(out_done, n + 1)
                dve.wait_ge(xb_made, n + 1)
                wait(dve, stored[u % 2], 16 * (2 * i + u // 2))
                dve.tensor_tensor(ost[:, u % 2, :], [ps[2], ps[3], ps[6], ps[7]][u][:, :], xg[:, u, :],
                                  ALU.add).then_inc(out_taken, 1)

            def group(i, last=False):
                def V(u):
                    if not last:
                        take_v(i + 1, u)
                soft(i, 0)
                soft(i, 1); turn_p(i, 0)
                soft(i, 2); turn_p(i, 1); normalise(i, 0)
                soft(i, 3); turn_p(i, 2); normalise(i, 1)
                V(0)
                turn_p(i, 3); normalise(i, 2); V(1)
                normalise(i, 3); V(2); V(3)
                if not last:
                    spread_q(i + 1, True)
                for u in range(NU):
                    mask_c2(i, u)
                route(i)
                weigh(i)
                for u in range(NU):
                    final(i, u)

            dve.wait_ge(preset, 3)
            for u in range(NU):
                take_v(0, u)
            spread_q(0, False)
            group(0)
            with dve.Fori(1, 7) as i:
                group(i)
            group(7, last=True)


def kernel(x, itok_B_78_3631, itok_B_0_7, itok_B_2182_4065, _lenS, L0_cond_log_dt, L0_cond_C, L0_cond_log_A_real,
           L0_cond_A_imag, L0_cond_D, L0_attn_Wq, L0_attn_bq, L0_attn_Wk, L0_attn_bk, L0_attn_Wv, L0_attn_bv,
           L0_cond2_W_sess, L0_cond2_b_sess, L0_cond2_W2, L0_cond2_b2, L0_ffn_W_base, L0_ffn_b_base,
           L0_ffn_W_router, L0_ffn_b_router, L0_ffn_lora_A, L0_ffn_lora_B):
    import concourse.bacc as _bacc
    from concourse import mybir as _mybir
    from concourse.bass_utils import run_bass_kernel_spmd as _run

    c_ = np.ascontiguousarray
    f4 = np.float32
    x = np.asarray(x)
    pi = np.arange(C).reshape(2, 2, 2, 4, 16).transpose(1, 3, 0, 2, 4).reshape(-1)

    def rows(a, n=128):
        return np.broadcast_to(np.asarray(a).reshape(1, -1), (n, np.asarray(a).size))

    def dup(a):
        t = np.asarray(a).T
        return np.concatenate([t, t], 0)

    xT = c_(x.reshape(B, T, LB, 128)[:, :, :, ::-1].transpose(1, 3, 2, 0).reshape(T, 128, C))
    xN = c_(x[:, :, pi].reshape(NG, NU, 4 * T, C).transpose(0, 2, 1, 3))
    Cm = np.asarray(L0_cond_C)
    bq = np.asarray(L0_attn_bq).reshape(4, 128).T
    bk = np.asarray(L0_attn_bk).reshape(2, 128).T
    bs = np.asarray(L0_cond2_b_sess).T
    pk = c_(np.concatenate([rows(L0_cond_log_dt), dup(L0_cond_log_A_real), dup(L0_cond_A_imag), dup(Cm[..., 0]),
                            dup(Cm[..., 1]), rows(L0_cond_D), bq, bk, np.concatenate([bs, bs], 0),
                            np.tile(np.asarray(L0_cond2_b2), 4).reshape(128, 1), rows(L0_ffn_b_router),
                            rows(np.asarray(L0_attn_bv).reshape(2, 2, 4, 16).transpose(1, 0, 2, 3)),
                            rows(np.asarray(L0_ffn_b_base)[pi])], 1))
    p = np.arange(128)
    ri = p // 64
    quarter = np.stack([1 - ri, 1 + ri, 2 + ri], 1).astype(np.float64)
    key, t = np.arange(T)[None, :], (p % T)[:, None]
    cst = c_(np.concatenate([
        quarter / 4, quarter * (np.pi / 2), p[:, None] + 128 * np.arange(LB)[None, :], (p % 32)[:, None],
        (p // 64)[:, None] == np.arange(2)[None, :], (p // 32)[:, None] == np.arange(4)[None, :],
        rows(np.arange(KK)), rows(KK * np.arange(KI)), np.where(key <= t, 0.0, -1e30), rows(pi), np.eye(128)],
        1).astype(f4))
    sid = np.asarray(itok_B_0_7)

    def by_bc(a):
        return np.repeat(np.asarray(a).reshape(32, 4).T, T, 0)

    ints = c_(np.concatenate([rows(itok_B_78_3631), by_bc(sid), by_bc(_lenS), by_bc(itok_B_2182_4065),
                              np.repeat(sid.reshape(64, 2).T, HID, 0)], 1))

    def blocks(w):
        return c_(np.asarray(w).reshape(LB, 128, -1).transpose(1, 0, 2))

    wq = blocks(np.asarray(L0_attn_Wq).T)
    wk = blocks(np.asarray(L0_attn_Wk).T)
    wv = blocks(np.asarray(L0_attn_Wv).reshape(2, 2, 4, 16, C).transpose(1, 0, 2, 3, 4).reshape(256, C).T)
    wsess = c_(np.asarray(L0_cond2_W_sess).transpose(1, 0, 2))
    wbase = blocks(np.asarray(L0_ffn_W_base)[pi][:, pi].T)
    la = np.asarray(L0_ffn_lora_A)[:, pi].transpose(1, 0, 2).reshape(C, 128)
    wsmall = blocks(np.concatenate([np.asarray(L0_ffn_W_router)[:, pi].T, la], 1))
    lorab = c_(np.asarray(L0_ffn_lora_B).reshape(128, C)[:, pi])

    nc = _bacc.Bacc("TRN2", target_bir_lowering=False, num_devices=1)
    arrays, args = {}, []
    for name, a in (("xT", xT), ("xN", xN), ("pk", pk), ("cst", cst), ("ints", ints), ("wq", wq), ("wk", wk),
                    ("wv", wv), ("wsess", wsess), ("w2", c_(np.asarray(L0_cond2_W2))), ("wbase", wbase),
                    ("wsmall", wsmall), ("lorab", lorab)):
        arrays[name] = a
        args.append(nc.dram_tensor(name, a.shape, _mybir.dt.from_np(a.dtype), kind="ExternalInput").ap())
    out = nc.dram_tensor("out", (NG, 128, NU, C), _mybir.dt.float32, kind="ExternalOutput").ap()
    kpad = nc.dram_tensor("kpad", (32, PADW), _mybir.dt.float32, kind="Internal").ap()
    yspill = nc.dram_tensor("yspill", (NG, 128, LB, TOK), _mybir.dt.float32, kind="Internal").ap()
    adaln_attn_ffn(nc, *args, out, kpad, yspill)
    r = _run(nc, [arrays], core_ids=[0])
    o = np.asarray(r.results[0]["out"]).transpose(0, 2, 1, 3).reshape(B, T, C)
    inv = np.empty_like(pi)
    inv[pi] = np.arange(C)
    return c_(o[:, :, inv])
```

```python
from contextlib import ExitStack

import numpy as np
import concourse.bass as bass
from concourse import mybir

F32 = mybir.dt.float32
I32 = mybir.dt.int32
ALU = mybir.AluOpType
ACT = mybir.ActivationFunctionType
AX = mybir.AxisListType.X

B, T, C = 128, 32, 512
LB = C // 128
NG = 8
GB = B // NG
NU = GB // 4
TOK = GB * T
NMODE = 64
NSESS, HID = 8, 64
NEXP, RANK = 8, 16
KI, KK = 16, 32
PADW = 640
VW = 17
SCALE = float(1.0 / np.sqrt(np.float32(32)))
MAGIC = 12582912.0
LOG2E = 1.4426950408889634
LN2_HI, LN2_LO = 0.693359375, -2.12194440e-4
INV2PI = 0.15915494309189535
TP1 = 6.28125
TP2 = 6.283185307179586 - TP1
PI_LO = 3.1415925

PCOL, CCOL, ICOL = {}, {}, {}


def _cols(table, spec):
    at = 0
    for name, n in spec:
        table[name] = (at, at + n)
        at += n
    return at


PW = _cols(PCOL, [("logs", 64), ("aimag", 32), ("cre", 32), ("cim", 32), ("dskip", 32), ("bq", 4), ("bk", 2),
                  ("bsess", NSESS), ("b2", 1), ("brout", NEXP), ("bv", 256), ("bbase", C)])
CW = _cols(CCOL, [("turn", 3), ("angle", 3), ("lpos", LB), ("cpos", 1), ("evenodd", 2), ("own", 4),
                  ("kvec", KK), ("ivec", KI), ("causal", T), ("tpos", C), ("ident", 128)])
IW = _cols(ICOL, [("length", B), ("sid_bc", 32), ("chans", 32), ("seq", 32), ("sid_ph", 64)])


def wait(eng, sem, value):
    if isinstance(value, int) and value <= 0:
        return
    eng.wait_ge(sem, value)


def adaln_attn_ffn(nc, xT, xN, pk, cst, ints, wq, wk, wv, wsess, w2, wbase, wsmall, lorab, out, kpad, yspill):
    with ExitStack() as ctx:
        def sb(name, shape, dt=F32):
            return ctx.enter_context(nc.sbuf_tensor(name, shape, dt))

        def sem(name):
            return ctx.enter_context(nc.semaphore(name))

        P_ = sb("params", [128, PW])
        K_ = sb("consts", [128, CW])
        If = sb("ints_f", [128, IW])
        wq_s = sb("wq_s", [128, LB, C])
        wk_s = sb("wk_s", [128, LB, 256])
        wv_s = sb("wv_s", [128, LB, 256])
        wbase_s = sb("wbase_s", [128, LB, C])
        wsmall_s = sb("wsmall_s", [128, LB, 136])
        lorab_s = sb("lorab_s", [128, C])
        wsel = sb("wsel", [128, NG * NU, HID])
        w2bd = sb("w2bd", [128, 64])
        bsel = sb("bsel", [128, 64])
        wbd = sb("wbd", [128, NU, 256])
        bsg = sb("bsg", [128, 8])
        seqg = sb("seqg", [128, NU])
        ybuf = sb("ybuf", [128, LB, TOK])
        q_st = sb("q_st", [128, 4, TOK])
        k_st = sb("k_st", [128, 2, TOK])
        v_st = sb("v_st", [128, NU, 2, 8 * VW])
        kbd = sb("kbd", [128, 2, 4, TOK])
        vbd = sb("vbd", [128, NU, 4, 4, 8 * VW])
        hsm = sb("hsm", [128, NU, 136])
        c2s = sb("c2s", [128, 2, C])
        c2m = sb("c2m", [128, 2, C])
        rinv = sb("rinv", [128, 2, 16])
        rmax = sb("rmax", [128, 2, 32])
        hwT = sb("hwT", [128, NU, 128])
        ost = sb("ost", [128, 2, C])
        rt = sb("rt", [128, 8, NU * NEXP])
        pair = sb("pair", [128, 2, NU * 64])
        big = sb("big", [128, 16384])
        yT = big[:, :].rearrange("p (l b h) -> p l b h", l=LB, b=B)
        yG = big[:, :].rearrange("p (l g t) -> p l g t", l=LB, g=NG)
        S = big[:, 0:2048].rearrange("p (s n) -> p s n", s=2)
        ET = big[:, 2048:4096].rearrange("p (s n) -> p s n", s=2)
        x1 = big[:, 4096:6144].rearrange("p (u n) -> p u n", u=NU)
        xg = big[:, 6144:8192].rearrange("p (u n) -> p u n", u=NU)
        c2T = big[:, 8192:10240].rearrange("p (u c n) -> p u c n", u=NU, c=LB)
        gel = big[:, 12288:14336].rearrange("p (s q n) -> p s q n", s=2, q=2)
        qbd = [big[:, a:a + 2048].rearrange("p (b q t) -> p b q t", b=GB, q=4) for a in (10240, 14336)]
        modes = kbd[:, :, :, :].rearrange("p a b c -> p (a b c)")
        ang = vbd[:, :, :, :, :].rearrange("p a b c d -> p (a b c d)")
        wall_s = ang[:, 7968:8480].rearrange("p (s n) -> p s n", s=NSESS)
        hflat = hsm[:, :, :].rearrange("p u n -> p (u n)")
        ohs = hflat[:, 0:256].rearrange("p (s u) -> p s u", s=NSESS)
        I_ = hflat[:, 256:256 + IW].bitcast(I32)
        toep = [modes[:, C * k:C * k + C] for k in range(4)]
        xs = [ybuf[:, k, :] for k in range(4)]
        lmask = wbd[:, 0:2, :].rearrange("p u n -> p (u n)").rearrange("p (l b) -> p l b", l=LB)
        hw = c2s[:, 0, :].rearrange("p (u n) -> p u n", u=NU)

        ps = [ctx.enter_context(nc.psum_tensor(f"ps{i}", [128, 512], F32)) for i in range(8)]

        def par(name, lo=0, hi=128):
            a, b = PCOL[name]
            return P_[lo:hi, a:b]

        def con(name, lo=0, hi=128):
            a, b = CCOL[name]
            return K_[lo:hi, a:b]

        def num(name):
            a, b = ICOL[name]
            return If[:, a:b]

        names = """params_in ints_in wsess_in w2_in weights_in setup dve_step w2_zero pool_step wsel_made
            modes_made grown tanh_made exps_made divided angles_made sines_made coef_made modes_ready kern_done kern_sb kpad_in
            conv_done conv_taken y_spilled y_in proj_done qk_taken v_taken qbd_made kbd_in vbd_in preset
            scores_done scores_taken row_max shifted exp_done transposed attn_done rsum_inv norm_taken
            x_in x1_made xb_made wbd_made h_done gelu_done c2_done c2_taken masked tr_done tr_taken
            small_done small_taken row_zt router_step hw_made hwT_done hwT_taken out_done out_taken""".split()
        s = {n: sem(n) for n in names}
        (params_in, ints_in, wsess_in, w2_in, weights_in, setup, dve_step, w2_zero, pool_step, wsel_made,
         modes_made, grown, tanh_made, exps_made, divided, angles_made, sines_made, coef_made, modes_ready, kern_done, kern_sb, kpad_in,
         conv_done, conv_taken, y_spilled, y_in, proj_done, qk_taken, v_taken, qbd_made, kbd_in, vbd_in, preset,
         scores_done, scores_taken, row_max, shifted, exp_done, transposed, attn_done, rsum_inv, norm_taken,
         x_in, x1_made, xb_made, wbd_made, h_done, gelu_done, c2_done, c2_taken, masked, tr_done, tr_taken,
         small_done, small_taken, row_zt, router_step, hw_made, hwT_done, hwT_taken, out_done, out_taken) = [s[n] for n in names]
        toep_in = [sem(f"toep_in{k}") for k in range(4)]
        xs_in = [sem(f"xs_in{k}") for k in range(4)]
        stored = [sem(f"stored{k}") for k in range(2)]

        NV, NU_ = 32 * KK, 32 * KI
        v0, u0, u1, end = 96, 96 + NV, 96 + NV + NU_, 96 + NV + 2 * NU_
        th = modes[:, 0:96]
        thV = modes[:, 96:96 + NV]
        thU = modes[:, 96 + NV:96 + NV + NU_]
        expV = modes[:, 1632:1632 + NV]
        expU = modes[:, 1632 + NV:1632 + NV + NU_]
        red = ang[:, 0:end]
        tmpa = ang[:, end:2 * end]
        snb = ang[:, 2 * end:3 * end]
        ucr = ang[:, 3 * end:3 * end + NU_]
        uci = ang[:, 3 * end + NU_:3 * end + 2 * NU_]
        L_ = q_st[:, 0, :]
        R_ = q_st[:, 1:3, :].rearrange("p a b -> p (a b)")
        tU = modes[:, 3168:4096]
        ksb = k_st[0:KI, :, :].rearrange("p a b -> p (a b)")
        zrow = c2m[0:32, 0, 0:128]

        def small(n):
            return tU[:, 32 * n:32 * n + 32]

        def small2(n):
            return tU[:, 32 * n:32 * n + 64]

        def over_n(a, n):
            return a.rearrange("p (h o) -> p h o", o=1).broadcast_to([128, 32, n])

        def outer(eng, o, a, vec, n):
            return eng.tensor_tensor(o.rearrange("p (h n) -> p h n", h=32), over_n(a, n),
                                     con(vec).rearrange("p (o n) -> p o n", o=1).broadcast_to([128, 32, n]), ALU.mult)

        block = ctx.enter_context(nc.Block())

        @block.sync
        def _(sp):
            sp.dma_start(P_[:, :], pk).then_inc(params_in, 16)
            sp.dma_start(K_[:, :], cst).then_inc(params_in, 16)
            sp.dma_start(I_[:, :], ints).then_inc(ints_in, 16)

            def load_x(t, k):
                if not isinstance(t, int) or t > 0:
                    sp.wait_ge(conv_done, 4 * t + k - 3)
                    sp.wait_ge(ints_in, 16)
                sp.dma_start(xs[k], xT[4 * t + k]).then_inc(xs_in[k], 16)

            for k in range(4):
                load_x(0, k)
            sp.dma_start(wq_s[:, :, :], wq).then_inc(weights_in, 16)
            sp.dma_start(wk_s[:, :, :], wk).then_inc(weights_in, 16)
            sp.dma_start(wv_s[:, :, :], wv).then_inc(weights_in, 16)
            sp.dma_start(wbase_s[:, :, :], wbase).then_inc(weights_in, 16)
            sp.dma_start(wsmall_s[:, :, :], wsmall).then_inc(weights_in, 16)
            sp.dma_start(lorab_s[:, :], lorab).then_inc(weights_in, 16)
            with sp.Fori(1, 8) as t:
                for k in range(4):
                    load_x(t, k)
            sp.wait_ge(conv_taken, 32)
            sp.dma_start(ybuf[:, :, :], yG[:, :, 1, :]).then_inc(y_in, 16)
            for g in range(2, NG):
                sp.dma_start(yspill[g], yG[:, :, g, :]).then_inc(y_spilled, 16)

            def place_k(j, waits):
                if waits:
                    wait(sp, scores_done, 8 * j)
                wait(sp, qk_taken, 6 * j + 6)
                for e in range(2):
                    for r in range(4):
                        p = 64 * e + 16 * r
                        sp.dma_start(kbd[p:p + 16, :, r, :], k_st[p:p + 16, :, :]).then_inc(kbd_in, 16)

            def place_v(j, waits):
                wait(sp, v_taken, 4 * j + 4)
                if waits:
                    wait(sp, attn_done, 8 * j)
                for b in range(4):
                    for ge in range(4):
                        sp.dma_start(vbd[32 * ge:32 * ge + 32, :, b, ge, :],
                                     v_st[32 * b:32 * b + 32, :, ge % 2, :]).then_inc(vbd_in, 16)

            def load_y(j):
                wait(sp, proj_done, 10 * j)
                sp.wait_ge(y_spilled, 16 * (NG - 2))
                sp.dma_start(ybuf[:, :, :], yspill[j]).then_inc(y_in, 16)

            sp.wait_ge(preset, 3)
            place_k(0, False)
            place_v(0, False)
            sp.wait_ge(y_spilled, 16 * (NG - 2))
            sp.wait_ge(y_in, 16)
            for u in range(NU):
                sp.dma_start(xg[:, u, :], xN[0, :, u, :]).then_inc(x_in, 16)

            def group(i, more_y, more):
                if more:
                    place_k(i + 1, True)
                    place_v(i + 1, True)
                if more_y:
                    load_y(i + 2)
                for u in range(NU):
                    sp.wait_ge(out_taken, 4 * i + u + 1)
                    sp.wait_ge(ints_in, 16)
                    sp.dma_start(out[i, :, u, :], ost[:, u % 2, :]).then_inc(stored[u % 2], 16)
                    if more:
                        sp.dma_start(xg[:, u, :], xN[i + 1, :, u, :]).then_inc(x_in, 16)

            group(0, True, True)
            with sp.Fori(1, 6) as i:
                group(i, True, True)
            group(6, False, True)
            group(7, False, False)
            sp.wait_ge(stored[0], 16 * 2 * NG)
            sp.wait_ge(stored[1], 16 * 2 * NG)

        @block.tensor
        def _(pe):
            pe.wait_ge(modes_ready, 1)
            for h in range(32):
                mm = pe.matmul(ps[6 + h // 16][0:KI, h % 16 * KK:(h % 16 + 1) * KK], L_[:, h * KI:(h + 1) * KI],
                               R_[:, h * KK:(h + 1) * KK], start=True, stop=True)
            mm.then_inc(kern_done, 1)

            def conv(t, k):
                pe.wait_ge(toep_in[k], 16 * t + 16)
                pe.wait_ge(xs_in[k], 16 * t + 16)
                if not isinstance(t, int) or t > 0:
                    pe.wait_ge(conv_taken, 4 * t + k - 3)
                for d in range(LB):
                    mm = pe.matmul(ps[k][:, 128 * d:512], toep[k][:, 128 * d:128 * d + 128],
                                   xs[k][:, 0:512 - 128 * d], start=(d == 0), stop=(d == LB - 1))
                mm.then_inc(conv_done, 1)

            for k in range(4):
                conv(0, k)
            with pe.Fori(1, 8) as t:
                for k in range(4):
                    conv(t, k)

            def project(j, c):
                bank = ps[4 + c % 2]
                first = isinstance(j, int) and j == 0
                y = yG[:, :, 0, :] if first else ybuf
                if c == 0 and not first:
                    pe.wait_ge(y_in, 16 * j)
                    wait(pe, small_taken, 4 * (j - 1))
                elif 2 <= c <= 7:
                    pe.wait_ge(qk_taken, 6 * j + c - 1)
                elif c >= 8:
                    pe.wait_ge(v_taken, 4 * j + c - 7)
                for l in range(LB):
                    f = dict(start=(l == 0), stop=(l == LB - 1))
                    if c < 4:
                        mm = pe.matmul(bank[:, :], wq_s[:, l, 128 * c:128 * c + 128], y[:, l, :], **f)
                    elif c < 6:
                        mm = pe.matmul(bank[:, :], wk_s[:, l, 128 * (c - 4):128 * (c - 3)], y[:, l, :], **f)
                    else:
                        u = c - 6
                        mm = pe.matmul(bank[:, 0:256], y[:, l, 128 * u:128 * u + 128], wv_s[:, l, :], **f)
                mm.then_inc(proj_done, 1)

            def scores(i, u):
                n = 4 * i + u
                if u == 0:
                    pe.wait_ge(qbd_made, 8 * i + 8)
                    pe.wait_ge(kbd_in, 16 * 8 * (i + 1))
                    wait(pe, hwT_taken, i)
                    wait(pe, tr_taken, 4 * i)
                for k in range(2):
                    wait(pe, scores_taken, 2 * n + k - 1)
                    for b in (4 * u + 2 * k, 4 * u + 2 * k + 1):
                        for f in range(2):
                            at = 256 * (b % 2) + 128 * f
                            mm = pe.matmul(ps[k][:, at:at + 128], qbd[f][:, b, :, :],
                                           kbd[:, f, :, 32 * b:32 * b + 32], start=True, stop=True)
                    mm.then_inc(scores_done, 1)

            def attend(i, u):
                n = 4 * i + u
                if u == 0:
                    pe.wait_ge(vbd_in, 16 * 16 * (i + 1))
                    wait(pe, out_taken, 4 * i)
                pe.wait_ge(transposed, n + 1)
                for f in range(2):
                    wait(pe, norm_taken, 2 * n + f - 1)
                    for b in range(4):
                        for r in range(4):
                            at = 256 * b + 128 * f + 32 * r
                            v = (4 * f + r) * VW
                            mm = pe.matmul(ps[2 + f][32 * b:32 * b + 32, 68 * r:68 * r + 68],
                                           ET[:, u % 2, at:at + 32], vbd[:, u, b, :, v:v + VW],
                                           start=True, stop=True)
                    mm.then_inc(attn_done, 1)

            def cond_h(i, u):
                n = 4 * i + u
                pe.wait_ge(x1_made, n + 1)
                if u == 0:
                    pe.wait_ge(wbd_made, 6 * i + 6)
                for p in range(2):
                    wait(pe, gelu_done, 2 * n + p - 1)
                    pe.matmul(ps[6 + p][:, :], wbd[:, u, 128 * p:128 * p + 128], x1[:, u, :],
                              start=True, stop=True).then_inc(h_done, 1)

            def cond_out(i, u):
                n = 4 * i + u
                pe.wait_ge(gelu_done, 2 * n + 2)
                if u == 0:
                    pe.wait_ge(scores_taken, 8 * i + 8)
                wait(pe, c2_taken, n)
                for p in range(2):
                    mm = pe.matmul(ps[0][64 * p:64 * p + 64, :], w2bd[:, :], gel[:, u % 2, p, :],
                                   start=True, stop=True)
                mm.then_inc(c2_done, 1)

            def turn(i, u):
                n = 4 * i + u
                pe.wait_ge(masked, n + 1)
                wait(pe, tr_taken, n)
                for c in range(LB):
                    mm = pe.transpose(ps[1][:, 128 * c:128 * c + 128], c2m[:, u % 2, 128 * c:128 * c + 128],
                                      con("ident"))
                mm.then_inc(tr_done, 1)

            def router_lora(i, u, last):
                n = 4 * i + u
                pe.wait_ge(tr_taken, n + 1)
                if u < 2:
                    pe.wait_ge(v_taken, 4 * i + (4 if last else 8))
                else:
                    pe.wait_ge(small_taken, n - 1)
                for c in range(LB):
                    mm = pe.matmul(ps[4 + u % 2][:, 0:136], c2T[:, u, c, :], wsmall_s[:, c, :],
                                   start=(c == 0), stop=(c == LB - 1))
                mm.then_inc(small_done, 1)

            out_bank = [ps[2], ps[3], ps[6], ps[7]]

            def base(i, u):
                if u == 0:
                    pe.wait_ge(norm_taken, 8 * i + 8)
                if u == 2:
                    pe.wait_ge(gelu_done, 8 * i + 8)
                for c in range(LB):
                    pe.matmul(out_bank[u][:, :], c2T[:, u, c, :], wbase_s[:, c, :], start=(c == 0), stop=False)

            def turn_h(i):
                pe.wait_ge(hw_made, i + 1)
                pe.wait_ge(c2_taken, 4 * i + 4)
                for u in range(NU):
                    mm = pe.transpose(ps[0][:, 128 * u:128 * u + 128], hw[:, u, :], con("ident"))
                mm.then_inc(hwT_done, 1)

            def expert(i, u):
                if u == 0:
                    pe.wait_ge(hwT_taken, i + 1)
                pe.matmul(out_bank[u][:, :], hwT[:, u, :], lorab_s[:, :], start=False, stop=True).then_inc(out_done, 1)

            def group(i, last=False):
                def A(c):
                    if not last:
                        project(i + 1, c)
                scores(i, 0); A(0)
                scores(i, 1); A(1); attend(i, 0); A(2)
                scores(i, 2); A(3); attend(i, 1); A(4)
                scores(i, 3); A(5); attend(i, 2); A(6); A(7)
                attend(i, 3); A(8); A(9)
                for k in range(NU + 3):
                    if k < NU:
                        cond_h(i, k)
                    if 1 <= k <= NU:
                        cond_out(i, k - 1)
                    if 2 <= k <= NU + 1:
                        turn(i, k - 2)
                    if k >= 3:
                        router_lora(i, k - 3, last)
                base(i, 0); base(i, 1)
                turn_h(i)
                base(i, 2)
                expert(i, 0); expert(i, 1); expert(i, 2)
                base(i, 3)
                expert(i, 3)

            pe.wait_ge(weights_in, 16 * 6)
            pe.wait_ge(conv_taken, 32)
            for c in range(10):
                project(0, c)
            pe.wait_ge(w2_in, 32)
            group(0)
            with pe.Fori(1, 7) as i:
                group(i)
            group(7, last=True)

        @block.scalar
        def _(act):
            for q in range(4):
                act.dma_start(wall_s[32 * q:32 * q + 32, :, :], wsess).then_inc(wsess_in, 16)
            act.wait_ge(w2_zero, 1)
            for p in range(2):
                act.dma_start(w2bd[64 * p:64 * p + 64, 32 * p:32 * p + 32], w2).then_inc(w2_in, 16)
            act.wait_ge(modes_made, 1)
            act.activation(small(6), small(5), ACT.Tanh, scale=0.5).then_inc(tanh_made, 1)
            act.wait_ge(grown, 2)
            act.activation(expV, expV, ACT.Exp).then_inc(exps_made, 1)
            act.activation(expU, expU, ACT.Exp).then_inc(exps_made, 1)
            act.wait_ge(angles_made, 1)
            act.activation(snb[:, 0:v0], red[:, 0:v0], ACT.Sin).then_inc(sines_made, 1)
            act.wait_ge(angles_made, 2)
            act.activation(snb[:, v0:end], red[:, v0:end], ACT.Sin).then_inc(sines_made, 1)
            act.wait_ge(kern_sb, 2)
            act.dma_start(kpad[:, 0:127], zrow[:, 0:127]).then_inc(kpad_in, 16)
            act.dma_start(kpad[:, 127:127 + C].rearrange("h (i k) -> i h k", k=KK),
                          ksb.rearrange("i (h k) -> i h k", k=KK)).then_inc(kpad_in, 16)
            act.wait_ge(kpad_in, 32)

            def load_toep(t, k):
                if not isinstance(t, int) or t > 0:
                    act.wait_ge(conv_done, 4 * t + k - 3)
                    act.wait_ge(kpad_in, 32)
                rows = bass.AP(kpad.tensor, (4 * t + k) * PADW + kpad.offset, [[1, 128], [1, C]])
                act.dma_start(toep[k], rows).then_inc(toep_in[k], 16)

            for k in range(4):
                load_toep(0, k)
            with act.Fori(1, 8) as t:
                for k in range(4):
                    load_toep(t, k)

            def take(j, c):
                act.wait_ge(proj_done, 10 * j + c + 1)
                if c == 0:
                    wait(act, qbd_made, 8 * j)
                if c == 4:
                    wait(act, kbd_in, 16 * 8 * j)
                if c < 4:
                    act.activation(q_st[:, c, :], ps[4 + c % 2][:, :], ACT.Identity,
                                   bias=par("bq")[:, c:c + 1]).then_inc(qk_taken, 1)
                else:
                    act.activation(k_st[:, c - 4, :], ps[4 + c % 2][:, :], ACT.Identity,
                                   bias=par("bk")[:, c - 4:c - 3]).then_inc(qk_taken, 1)

            def expo(i, u):
                act.wait_ge(shifted, 4 * i + u + 1)
                act.activation(S[:, u % 2, :], S[:, u % 2, :], ACT.Exp, scale=SCALE).then_inc(exp_done, 1)

            def gelu(i, u, p):
                n = 4 * i + u
                act.wait_ge(h_done, 2 * n + p + 1)
                wait(act, c2_done, n - 1)
                act.activation(gel[:, u % 2, p, :], ps[6 + p][:, :], ACT.Gelu,
                               bias=bsg[:, 2 * u + p:2 * u + p + 1]).then_inc(gelu_done, 1)

            def take_c2(i, u):
                n = 4 * i + u
                act.wait_ge(c2_done, n + 1)
                wait(act, masked, n - 1)
                act.activation(c2s[:, u % 2, :], ps[0][:, :], ACT.Identity, bias=par("b2")).then_inc(c2_taken, 1)

            def take_turned(i, u):
                act.wait_ge(tr_done, 4 * i + u + 1)
                wait(act, out_done, 4 * i)
                act.activation(c2T[:, u, :, :], ps[1][:, :].rearrange("p (c n) -> p c n", c=LB),
                               ACT.Copy).then_inc(tr_taken, 1)

            def take_small(i, u):
                act.wait_ge(small_done, 4 * i + u + 1)
                wait(act, hw_made, i)
                act.activation(hsm[:, u, :], ps[4 + u % 2][:, 0:136], ACT.Copy).then_inc(small_taken, 1)

            def take_hw(i):
                act.wait_ge(hwT_done, i + 1)
                wait(act, out_done, 4 * i)
                act.activation(hwT[:, :, :], ps[0][:, :].rearrange("p (u n) -> p u n", u=NU),
                               ACT.Copy).then_inc(hwT_taken, 1)

            def group(i, last=False):
                def A(c):
                    if not last:
                        take(i + 1, c)
                expo(i, 0); A(0)
                expo(i, 1); A(1); A(2)
                expo(i, 2); A(3); A(4)
                expo(i, 3); A(5)
                for k in range(NU + 3):
                    if k < NU:
                        gelu(i, k, 0); gelu(i, k, 1)
                    if 1 <= k <= NU:
                        take_c2(i, k - 1)
                    if 2 <= k <= NU + 1:
                        take_turned(i, k - 2)
                    if k >= 3:
                        take_small(i, k - 3)
                take_hw(i)

            act.wait_ge(wsel_made, 1)
            for c in range(6):
                take(0, c)
            group(0)
            with act.Fori(1, 7) as i:
                group(i)
            group(7, last=True)

        @block.gpsimd
        def _(pool):
            steps = [0]

            def step(ins):
                steps[0] += 1
                ins.then_inc(pool_step, 1)
                pool.wait_ge(pool_step, steps[0])

            pool.memset(w2bd[:, :], 0.0).then_inc(w2_zero, 1)
            pool.wait_ge(modes_made, 1)
            outer(pool, expV, small(5), "kvec", KK).then_inc(grown, 1)
            outer(pool, expU, small(5), "ivec", KI).then_inc(grown, 1)
            def mul(o, a, b, op=ALU.mult):
                step(pool.tensor_tensor(o, a, b, op))

            em, er, ei, t0, t1, nr, ni = small(0), small(1), small(7), small(10), small(11), small(12), small(13)
            am, ai, cre, cim = small(9), par("aimag"), par("cre"), par("cim")
            sn, cs, sh = snb[:, 0:32], snb[:, 32:64], snb[:, 64:96]
            pool.wait_ge(divided, 1)
            pool.wait_ge(sines_made, 1)
            step(pool.tensor_scalar(t0, em, 1.0, 1.0, ALU.add, ALU.mult))
            mul(ei, t0, sn)
            mul(er, em, cs)
            mul(t0, sh, sh)
            step(pool.tensor_scalar(t0, t0, -2.0, 0.0, ALU.mult, ALU.add))
            mul(er, er, t0, ALU.add)
            mul(nr, cre, er)
            mul(t0, cim, ei)
            mul(nr, nr, t0, ALU.subtract)
            mul(ni, cre, ei)
            mul(t0, cim, er)
            mul(ni, ni, t0, ALU.add)
            mul(t0, nr, am)
            mul(t1, ni, ai)
            mul(t0, t1, t0, ALU.subtract)
            mul(t1, nr, ai)
            mul(nr, ni, am)
            mul(t1, t1, nr, ALU.add)
            mul(t0, t0, small(2))
            mul(t1, t1, small(3))
            pool.wait_ge(exps_made, 2)
            eU = expU.rearrange("p (h n) -> p h n", h=32)
            pool.tensor_tensor(ucr.rearrange("p (h n) -> p h n", h=32), eU, over_n(t0, KI), ALU.mult).then_inc(coef_made, 1)
            pool.tensor_tensor(uci.rearrange("p (h n) -> p h n", h=32), eU, over_n(t1, KI), ALU.mult).then_inc(coef_made, 1)
            pool.wait_ge(wsess_in, 64)
            pool.wait_ge(setup, 8)
            pool.wait_ge(kern_done, 1)
            tmp = q_st[:, :, :].rearrange("p a b -> p (a b)").rearrange("p (u n) -> p u n", u=32)
            for k in range(NSESS):
                dst = wsel[:, :, :] if k == 0 else tmp
                step(pool.tensor_tensor(dst, wall_s[:, k:k + 1, :].broadcast_to([128, 32, HID]),
                                        ohs[:, k, :].rearrange("p (u o) -> p u o", o=1).broadcast_to([128, 32, HID]),
                                        ALU.mult))
                if k:
                    ins = pool.tensor_tensor(wsel[:, :, :], wsel[:, :, :], tmp, ALU.add)
                    if k < NSESS - 1:
                        step(ins)
                    else:
                        ins.then_inc(wsel_made, 1)
            pool.wait_ge(wsel_made, 1)
            pool.wait_ge(conv_taken, 32)
            pool.memset(kbd[:, :, :, :], 0.0).then_inc(preset, 1)
            pool.memset(vbd[:, :, :, :, :], 0.0).then_inc(preset, 1)
            pool.memset(v_st[:, :, :, :], 1.0).then_inc(preset, 1)

            def residual(i, u):
                n = 4 * i + u
                if u == 0:
                    pool.wait_ge(x_in, 64 * i + 64)
                pool.wait_ge(norm_taken, 2 * n + 2)
                pool.tensor_tensor(x1[:, u, :], x1[:, u, :], xg[:, u, :], ALU.add).then_inc(x1_made, 1)
                pool.wait_ge(x1_made, n + 1)
                pool.tensor_tensor(xg[:, u, :], x1[:, u, :], par("bbase"), ALU.add).then_inc(xb_made, 1)

            def conditions(i):
                for u in range(NU):
                    w = wsel[:, 4 * i + u, :] if isinstance(i, int) else wsel[:, bass.ds(4 * i + u, 1), :]
                    w = w.rearrange("p n -> p () n") if isinstance(i, int) else w
                    pool.tensor_tensor(wbd[:, u, :].rearrange("p (b n) -> p b n", b=4),
                                       w.broadcast_to([128, 4, HID]),
                                       con("own").rearrange("p (b o) -> p b o", o=1).broadcast_to([128, 4, HID]),
                                       ALU.mult).then_inc(wbd_made, 1)
                pool.tensor_copy(bsg[:, :], bsel[:, bass.ds(8 * i, 8)]).then_inc(wbd_made, 1)
                a = ICOL["seq"][0]
                pool.tensor_copy(seqg[:, :], If[:, bass.ds(a + 4 * i, 4)]).then_inc(wbd_made, 1)

            def group(i):
                residual(i, 0)
                conditions(i)
                for u in range(1, NU):
                    residual(i, u)

            pool.wait_ge(setup, 10)
            group(0)
            with pool.Fori(1, 8) as i:
                group(i)

        @block.vector
        def _(dve):
            steps = [0]

            def step(ins):
                steps[0] += 1
                ins.then_inc(dve_step, 1)
                dve.wait_ge(dve_step, steps[0])

            def tt(o, a, b, op):
                step(dve.tensor_tensor(o, a, b, op))

            def ts(o, a, s1, op0, s2=None, op1=None):
                if s2 is None:
                    step(dve.tensor_scalar(o, a, s1, None, op0))
                else:
                    step(dve.tensor_scalar(o, a, s1, s2, op0, op1))

            def stt(o, a, sc, b, op0, op1):
                step(dve.scalar_tensor_tensor(out=o, in0=a, scalar=sc, in1=b, op0=op0, op1=op1))

            dve.wait_ge(params_in, 32)
            dve.memset(zrow, 0.0).then_inc(kern_sb, 1)
            X, N_, R, PL = par("logs"), small2(0), small2(2), small2(8)
            ts(N_, X, LOG2E, ALU.mult, MAGIC, ALU.add)
            ts(N_, N_, MAGIC, ALU.subtract)
            stt(R, N_, -LN2_HI, X, ALU.mult, ALU.add)
            stt(R, N_, -LN2_LO, R, ALU.mult, ALU.add)
            ts(PL, R, 1.0 / 5040, ALU.mult)
            for c in (1.0 / 720, 1.0 / 120, 1.0 / 24, 1.0 / 6, 0.5, 1.0):
                stt(PL, PL, c, R, ALU.add, ALU.mult)
            ts(PL, PL, 1.0, ALU.add)
            ts(N_, N_, 127.0, ALU.add, 8388608.0, ALU.mult)
            step(dve.tensor_copy(R.bitcast(I32), N_))
            tt(PL, PL, R, ALU.mult)
            dt, am = small(8), small(9)
            dr = small(5)
            stt(dr, am, -1.0, dt, ALU.mult, ALU.mult)
            dve.tensor_tensor(th[:, 0:32], par("aimag"), dt, ALU.mult).then_inc(modes_made, 1)
            dve.wait_ge(modes_made, 1)
            ts(th[:, 32:64], th[:, 0:32], 1.0, ALU.mult)
            ts(th[:, 64:96], th[:, 0:32], 0.5, ALU.mult)
            turn, angle = con("turn"), con("angle")

            def reduce_angles(lo, hi, parts):
                for a, q, _w, b, e in parts:
                    ts(tmpa[:, b:e], a, INV2PI, ALU.mult, q, ALU.add)
                ts(tmpa[:, lo:hi], tmpa[:, lo:hi], MAGIC, ALU.add)
                ts(tmpa[:, lo:hi], tmpa[:, lo:hi], MAGIC, ALU.subtract)
                for a, _q, _w, b, e in parts:
                    stt(red[:, b:e], tmpa[:, b:e], -TP1, a, ALU.mult, ALU.add)
                stt(red[:, lo:hi], tmpa[:, lo:hi], -TP2, red[:, lo:hi], ALU.mult, ALU.add)
                for _a, _q, w, b, e in parts:
                    ts(red[:, b:e], red[:, b:e], w, ALU.add, PI_LO, ALU.min)
                dve.tensor_scalar(red[:, lo:hi], red[:, lo:hi], -PI_LO, None, ALU.max).then_inc(angles_made, 1)

            reduce_angles(0, 96, [(th[:, 0:32], 0.0, 0.0, 0, 32), (th[:, 32:64], 0.25, float(np.pi / 2), 32, 64),
                                  (th[:, 64:96], 0.0, 0.0, 64, 96)])
            ai, tn, em, den, t0 = par("aimag"), small(6), small(0), small(3), small(7)
            tt(t0, am, am, ALU.mult)
            tt(den, ai, ai, ALU.mult)
            tt(den, den, t0, ALU.add)
            step(dve.reciprocal(den, den))
            ts(small(2), den, 2.0, ALU.mult)
            ts(small(3), den, -2.0, ALU.mult)
            dve.wait_ge(tanh_made, 1)
            ts(t0, tn, -1.0, ALU.mult, 1.0, ALU.add)
            step(dve.reciprocal(t0, t0))
            dve.scalar_tensor_tensor(out=em, in0=tn, scalar=2.0, in1=t0, op0=ALU.mult, op1=ALU.mult).then_inc(divided, 1)
            step(outer(dve, thV, th[:, 0:32], "kvec", KK))
            step(outer(dve, thU, th[:, 0:32], "ivec", KI))
            reduce_angles(v0, end, [(thV, turn[:, 0:1], angle[:, 0:1], v0, u0), (thU, turn[:, 1:2], angle[:, 1:2], u0, u1),
                                    (thU, turn[:, 2:3], angle[:, 2:3], u1, end)])
            dve.wait_ge(exps_made, 2)
            dve.wait_ge(sines_made, 2)
            dve.wait_ge(coef_made, 2)
            tt(R_, expV, snb[:, v0:u0], ALU.mult)
            tt(tmpa[:, 0:NU_], uci, snb[:, u1:end], ALU.mult)
            tt(L_, ucr, snb[:, u0:u1], ALU.mult)
            dve.tensor_tensor(L_, L_, tmpa[:, 0:NU_], ALU.add).then_inc(modes_ready, 1)
            dve.wait_ge(kern_done, 1)
            step(dve.tensor_copy(ksb[:, 0:512], ps[6][0:KI, :]))
            step(dve.tensor_copy(ksb[:, 512:1024], ps[7][0:KI, :]))
            k0 = ksb[0:1, :].rearrange("p (h k) -> p h k", h=32)[:, :, 0]
            dve.tensor_tensor(k0, k0, par("dskip", 0, 1), ALU.add).then_inc(kern_sb, 1)

            dve.wait_ge(ints_in, 16)
            step(dve.tensor_copy(If[:, :], I_[:, :]))
            for l in range(LB):
                ts(lmask[:, l, :], num("length"), con("lpos")[:, l:l + 1], ALU.is_gt)
            cm = rmax[:, 0, :]
            ts(cm, num("chans"), con("cpos"), ALU.is_gt)
            for k in range(NSESS):
                dve.scalar_tensor_tensor(out=ohs[:, k, :], in0=num("sid_bc"), scalar=float(k), in1=cm,
                                         op0=ALU.is_equal, op1=ALU.mult).then_inc(setup, 1)
            bs = par("bsess")
            for k in range(NSESS):
                dst = bsel[:, :] if k == 0 else pair[:, 0, 0:64]
                ts(dst, num("sid_ph"), float(k), ALU.is_equal, bs[:, k:k + 1], ALU.mult)
                if k:
                    tt(bsel[:, :], bsel[:, :], pair[:, 0, 0:64], ALU.add)
            dve.tensor_copy(pair[:, 1, 0:64], bsel[:, :]).then_inc(setup, 1)
            dve.tensor_copy(pair[:, 1, 64:96], num("seq")).then_inc(setup, 1)

            def take_conv(t, k):
                dve.wait_ge(conv_done, 4 * t + k + 1)
                h = 4 * t + k
                o = yT[:, :, :, h] if isinstance(t, int) else yT[:, :, :, bass.ds(h, 1)].rearrange("p l b o -> p l (b o)")
                dve.tensor_tensor(o, ps[k][:, :].rearrange("p (l b) -> p l b", l=LB), lmask[:, :, :],
                                  ALU.mult).then_inc(conv_taken, 1)

            for k in range(4):
                take_conv(0, k)
            with dve.Fori(1, 8) as t:
                for k in range(4):
                    take_conv(t, k)

            causal = con("causal").rearrange("p (o n) -> p o n", o=1).broadcast_to([128, 16, T])

            def take_v(j, u):
                dve.wait_ge(proj_done, 10 * j + 7 + u)
                if u == 0:
                    wait(dve, vbd_in, 16 * 16 * j)
                dve.tensor_tensor(v_st[:, u, :, :].rearrange("p e (k w) -> p (e k) w", w=VW)[:, :, 0:16],
                                  ps[4 + u % 2][:, 0:256].rearrange("p (k w) -> p k w", w=16),
                                  par("bv").rearrange("p (k w) -> p k w", w=16), ALU.add).then_inc(v_taken, 1)

            def spread_q(j, waits):
                wait(dve, qk_taken, 6 * j + 4)
                if waits:
                    wait(dve, scores_done, 8 * j)
                else:
                    dve.wait_ge(y_spilled, 16 * (NG - 2))
                    dve.wait_ge(y_in, 16)
                for g in range(2):
                    for f in range(2):
                        for e in range(2):
                            dve.tensor_scalar(qbd[f][:, :, 2 * g + e, :],
                                              q_st[:, 2 * g + f, :].rearrange("p (b t) -> p b t", b=GB),
                                              con("evenodd")[:, e:e + 1], None, ALU.mult).then_inc(qbd_made, 1)

            def soft(i, u):
                n = 4 * i + u
                Su = S[:, u % 2, :]
                for k in range(2):
                    dve.wait_ge(scores_done, 2 * n + k + 1)
                    dve.tensor_tensor(Su[:, 512 * k:512 * k + 512].rearrange("p (m n) -> p m n", n=T),
                                      ps[k][:, :].rearrange("p (m n) -> p m n", n=T), causal,
                                      ALU.add).then_inc(scores_taken, 1)
                dve.wait_ge(scores_taken, 2 * n + 2)
                S3 = Su.rearrange("p (m n) -> p m n", n=T)
                dve.tensor_reduce(rmax[:, u % 2, :], S3, AX, ALU.max).then_inc(row_max, 1)
                dve.wait_ge(row_max, n + 1)
                dve.tensor_tensor(S3, S3, rmax[:, u % 2, :].rearrange("p (m o) -> p m o", o=1).broadcast_to([128, 32, T]),
                                  ALU.subtract).then_inc(shifted, 1)

            def turn_p(i, u):
                n = 4 * i + u
                dve.wait_ge(exp_done, n + 1)
                wait(dve, attn_done, 2 * n - 2)
                dve.transpose(ET[:, u % 2, :], S[:, u % 2, :]).then_inc(transposed, 1)

            def normalise(i, u):
                n = 4 * i + u
                for f in range(2):
                    dve.wait_ge(attn_done, 2 * n + f + 1)
                    pv = ps[2 + f][:, 0:16 * VW].rearrange("p (m w) -> p m w", w=VW)
                    dve.reciprocal(rinv[:, f, :], pv[:, :, 16]).then_inc(rsum_inv, 1)
                    if f == 0:
                        wait(dve, h_done, 8 * i)
                        wait(dve, xb_made, 4 * i)
                    dve.wait_ge(rsum_inv, 2 * n + f + 1)
                    dve.tensor_tensor(x1[:, u, 256 * f:256 * f + 256].rearrange("p (m w) -> p m w", w=16),
                                      pv[:, :, 0:16],
                                      rinv[:, f, :].rearrange("p (m o) -> p m o", o=1).broadcast_to([128, 16, 16]),
                                      ALU.mult).then_inc(norm_taken, 1)

            def mask_c2(i, u):
                n = 4 * i + u
                dve.wait_ge(c2_taken, n + 1)
                wait(dve, tr_done, n - 1)
                dve.scalar_tensor_tensor(out=c2m[:, u % 2, :], in0=con("tpos"), scalar=seqg[:, u:u + 1],
                                         in1=c2s[:, u % 2, :], op0=ALU.is_lt, op1=ALU.mult).then_inc(masked, 1)

            NR = 12

            def route(i):
                k = [0]

                def r(ins):
                    k[0] += 1
                    ins.then_inc(router_step, 1)
                    dve.wait_ge(router_step, NR * i + k[0])

                def t3(x):
                    return x.rearrange("p (u e) -> p u e", u=NU)

                z, ki, ci_, su, sz = (rt[:, m, :] for m in range(5))
                kz, tau = rt[:, 5, 0:NU], rt[:, 6, 0:NU]
                G = pair[:, 0, :].rearrange("p (m j) -> p m j", j=NEXP)
                GZ = pair[:, 1, :].rearrange("p (m j) -> p m j", j=NEXP)

                def ui(x):
                    return x.rearrange("p (m o) -> p m o", o=1).broadcast_to([128, NU * NEXP, NEXP])

                def uj(x):
                    return x.rearrange("p (u o e) -> p u o e", u=NU, o=1).broadcast_to([128, NU, NEXP, NEXP])

                def u4(x):
                    return x.rearrange("p (u i) j -> p u i j", u=NU)

                dve.wait_ge(small_taken, 4 * i + 4)
                r(dve.tensor_tensor(t3(z), hsm[:, :, 0:NEXP],
                                    par("brout").rearrange("p (o e) -> p o e", o=1).broadcast_to([128, NU, NEXP]),
                                    ALU.add))
                r(dve.tensor_tensor(u4(G), uj(z), u4(ui(z)), ALU.is_ge))
                r(dve.tensor_tensor(u4(GZ), u4(G), uj(z), ALU.mult))
                r(dve.tensor_reduce(ki, G, AX, ALU.add))
                r(dve.tensor_reduce(ci_, GZ, AX, ALU.add))
                r(dve.tensor_tensor(su, z, ki, ALU.mult))
                r(dve.scalar_tensor_tensor(out=su, in0=su, scalar=1.0, in1=ci_, op0=ALU.add, op1=ALU.is_gt))
                r(dve.tensor_tensor(sz, su, z, ALU.mult))
                r(dve.tensor_reduce(kz, t3(su), AX, ALU.add))
                r(dve.tensor_reduce(tau, t3(sz), AX, ALU.add))
                r(dve.reciprocal(kz, kz))
                r(dve.scalar_tensor_tensor(out=tau, in0=tau, scalar=-1.0, in1=kz, op0=ALU.add, op1=ALU.mult))
                assert k[0] == NR

            def weigh(i):
                z, zt, tau = rt[:, 0, :], rt[:, 7, :], rt[:, 6, 0:NU]
                dve.tensor_tensor(zt.rearrange("p (u e) -> p u e", u=NU), z.rearrange("p (u e) -> p u e", u=NU),
                                  tau.rearrange("p (u o) -> p u o", o=1).broadcast_to([128, NU, NEXP]),
                                  ALU.subtract).then_inc(row_zt, 1)
                dve.wait_ge(row_zt, 2 * i + 1)
                dve.tensor_scalar(zt, zt, 0.0, None, ALU.max).then_inc(row_zt, 1)
                wait(dve, hwT_done, i)
                dve.wait_ge(row_zt, 2 * i + 2)
                dve.tensor_tensor(hw[:, :, :].rearrange("p u (e r) -> p u e r", e=NEXP),
                                  hsm[:, :, NEXP:136].rearrange("p u (e r) -> p u e r", e=NEXP),
                                  zt.rearrange("p (u e o) -> p u e o", u=NU, o=1).broadcast_to([128, NU, NEXP, RANK]),
                                  ALU.mult).then_inc(hw_made, 1)

            def final(i, u):
                n = 4 * i + u
                dve.wait_ge(out_done, n + 1)
                dve.wait_ge(xb_made, n + 1)
                wait(dve, stored[u % 2], 16 * (2 * i + u // 2))
                dve.tensor_tensor(ost[:, u % 2, :], [ps[2], ps[3], ps[6], ps[7]][u][:, :], xg[:, u, :],
                                  ALU.add).then_inc(out_taken, 1)

            def group(i, last=False):
                def V(u):
                    if not last:
                        take_v(i + 1, u)
                soft(i, 0); turn_p(i, 0)
                soft(i, 1); turn_p(i, 1); normalise(i, 0)
                soft(i, 2); turn_p(i, 2); normalise(i, 1)
                soft(i, 3); turn_p(i, 3); normalise(i, 2)
                V(0); V(1)
                normalise(i, 3); V(2); V(3)
                if not last:
                    spread_q(i + 1, True)
                for u in range(NU):
                    mask_c2(i, u)
                route(i)
                weigh(i)
                for u in range(NU):
                    final(i, u)

            dve.wait_ge(preset, 3)
            for u in range(NU):
                take_v(0, u)
            spread_q(0, False)
            group(0)
            with dve.Fori(1, 7) as i:
                group(i)
            group(7, last=True)


def kernel(x, itok_B_78_3631, itok_B_0_7, itok_B_2182_4065, _lenS, L0_cond_log_dt, L0_cond_C, L0_cond_log_A_real,
           L0_cond_A_imag, L0_cond_D, L0_attn_Wq, L0_attn_bq, L0_attn_Wk, L0_attn_bk, L0_attn_Wv, L0_attn_bv,
           L0_cond2_W_sess, L0_cond2_b_sess, L0_cond2_W2, L0_cond2_b2, L0_ffn_W_base, L0_ffn_b_base,
           L0_ffn_W_router, L0_ffn_b_router, L0_ffn_lora_A, L0_ffn_lora_B):
    import concourse.bacc as _bacc
    from concourse import mybir as _mybir
    from concourse.bass_utils import run_bass_kernel_spmd as _run

    c_ = np.ascontiguousarray
    f4 = np.float32
    x = np.asarray(x)
    pi = np.arange(C).reshape(2, 2, 2, 4, 16).transpose(1, 3, 0, 2, 4).reshape(-1)

    def rows(a, n=128):
        return np.broadcast_to(np.asarray(a).reshape(1, -1), (n, np.asarray(a).size))

    def dup(a):
        t = np.asarray(a).T
        return np.concatenate([t, t], 0)

    xT = c_(x.reshape(B, T, LB, 128)[:, :, :, ::-1].transpose(1, 3, 2, 0).reshape(T, 128, C))
    xN = c_(x[:, :, pi].reshape(NG, NU, 4 * T, C).transpose(0, 2, 1, 3))
    Cm = np.asarray(L0_cond_C)
    bq = np.asarray(L0_attn_bq).reshape(4, 128).T
    bk = np.asarray(L0_attn_bk).reshape(2, 128).T
    bs = np.asarray(L0_cond2_b_sess).T
    pk = c_(np.concatenate([rows(L0_cond_log_dt), dup(L0_cond_log_A_real), dup(L0_cond_A_imag), dup(Cm[..., 0]),
                            dup(Cm[..., 1]), rows(L0_cond_D), bq, bk, np.concatenate([bs, bs], 0),
                            np.tile(np.asarray(L0_cond2_b2), 4).reshape(128, 1), rows(L0_ffn_b_router),
                            rows(np.asarray(L0_attn_bv).reshape(2, 2, 4, 16).transpose(1, 0, 2, 3)),
                            rows(np.asarray(L0_ffn_b_base)[pi])], 1))
    p = np.arange(128)
    ri = p // 64
    quarter = np.stack([1 - ri, 1 + ri, 2 + ri], 1).astype(np.float64)
    key, t = np.arange(T)[None, :], (p % T)[:, None]
    cst = c_(np.concatenate([
        quarter / 4, quarter * (np.pi / 2), p[:, None] + 128 * np.arange(LB)[None, :], (p % 32)[:, None],
        (p // 64)[:, None] == np.arange(2)[None, :], (p // 32)[:, None] == np.arange(4)[None, :],
        rows(np.arange(KK)), rows(KK * np.arange(KI)), np.where(key <= t, 0.0, -1e30), rows(pi), np.eye(128)],
        1).astype(f4))
    sid = np.asarray(itok_B_0_7)

    def by_bc(a):
        return np.repeat(np.asarray(a).reshape(32, 4).T, T, 0)

    ints = c_(np.concatenate([rows(itok_B_78_3631), by_bc(sid), by_bc(_lenS), by_bc(itok_B_2182_4065),
                              np.repeat(sid.reshape(64, 2).T, HID, 0)], 1))

    def blocks(w):
        return c_(np.asarray(w).reshape(LB, 128, -1).transpose(1, 0, 2))

    wq = blocks(np.asarray(L0_attn_Wq).T)
    wk = blocks(np.asarray(L0_attn_Wk).T)
    wv = blocks(np.asarray(L0_attn_Wv).reshape(2, 2, 4, 16, C).transpose(1, 0, 2, 3, 4).reshape(256, C).T)
    wsess = c_(np.asarray(L0_cond2_W_sess).transpose(1, 0, 2))
    wbase = blocks(np.asarray(L0_ffn_W_base)[pi][:, pi].T)
    la = np.asarray(L0_ffn_lora_A)[:, pi].transpose(1, 0, 2).reshape(C, 128)
    wsmall = blocks(np.concatenate([np.asarray(L0_ffn_W_router)[:, pi].T, la], 1))
    lorab = c_(np.asarray(L0_ffn_lora_B).reshape(128, C)[:, pi])

    nc = _bacc.Bacc("TRN2", target_bir_lowering=False, num_devices=1)
    arrays, args = {}, []
    for name, a in (("xT", xT), ("xN", xN), ("pk", pk), ("cst", cst), ("ints", ints), ("wq", wq), ("wk", wk),
                    ("wv", wv), ("wsess", wsess), ("w2", c_(np.asarray(L0_cond2_W2))), ("wbase", wbase),
                    ("wsmall", wsmall), ("lorab", lorab)):
        arrays[name] = a
        args.append(nc.dram_tensor(name, a.shape, _mybir.dt.from_np(a.dtype), kind="ExternalInput").ap())
    out = nc.dram_tensor("out", (NG, 128, NU, C), _mybir.dt.float32, kind="ExternalOutput").ap()
    kpad = nc.dram_tensor("kpad", (32, PADW), _mybir.dt.float32, kind="Internal").ap()
    yspill = nc.dram_tensor("yspill", (NG, 128, LB, TOK), _mybir.dt.float32, kind="Internal").ap()
    adaln_attn_ffn(nc, *args, out, kpad, yspill)
    r = _run(nc, [arrays], core_ids=[0])
    o = np.asarray(r.results[0]["out"]).transpose(0, 2, 1, 3).reshape(B, T, C)
    inv = np.empty_like(pi)
    inv[pi] = np.arange(C)
    return c_(o[:, :, inv])
```

```python
from contextlib import ExitStack

import numpy as np
import concourse.bass as bass
from concourse import mybir

F32 = mybir.dt.float32
F32R = mybir.dt.float32r
I32 = mybir.dt.int32
ALU = mybir.AluOpType
ACT = mybir.ActivationFunctionType
AX = mybir.AxisListType.X

B, T, C = 128, 32, 512
LB = C // 128
NG = 8
GB = B // NG
NU = GB // 4
TOK = GB * T
NSESS, HID = 8, 64
NEXP, RANK = 8, 16
KI, KK = 16, 32
PADW = 640
VW = 17
SCALE = float(1.0 / np.sqrt(np.float32(32)))
MAGIC = 12582912.0
LOG2E = 1.4426950408889634
LN2_HI, LN2_LO = 0.693359375, -2.12194440e-4
INV2PI = 0.15915494309189535
TP1 = 6.28125
TP2 = 6.283185307179586 - TP1
PI_LO = 3.1415925
PI_SAFE = 3.1415920

PCOL, CCOL, ICOL, SCOL = {}, {}, {}, {}


def _cols(table, spec):
    at = 0
    for name, n in spec:
        table[name] = (at, at + n)
        at += n
    return at


SW = _cols(SCOL, [("logs", 64), ("aimag", 32), ("cre", 32), ("cim", 32), ("dskip", 8), ("bsess", NSESS),
                  ("turn", 3), ("angle", 3), ("upper", 3), ("lower", 3), ("lpos", LB), ("cpos", 1),
                  ("kvec", KK), ("ivec", KI)])
PW = _cols(PCOL, [("bq", 4), ("bk", 2), ("b2", 32), ("brout", NEXP), ("bv", 256), ("bbase", C)])
CW = _cols(CCOL, [("evenodd", 2), ("own", 4), ("causal", T), ("chan", LB), ("ident", 128)])
IW = _cols(ICOL, [("length", B), ("sid_bc", 32), ("chans", 32), ("seq", B), ("sid_ph", 64)])


def wait(eng, sem, value):
    if isinstance(value, int) and value <= 0:
        return
    eng.wait_ge(sem, value)


def adaln_attn_ffn(nc, xT, xN, early, pk, cst, ints, wq, wk, wv, wsess, w2, wbase, wsmall, lorab,
                   out, kpad, yspill, vrows):
    with ExitStack() as ctx:
        def sb(name, shape, dt=F32):
            return ctx.enter_context(nc.sbuf_tensor(name, shape, dt))

        def sem(name):
            return ctx.enter_context(nc.semaphore(name))

        P_ = sb("params", [128, PW])
        K_ = sb("consts", [128, CW])
        wq_s = [sb(f"wq_{n}", [128, LB, C], F32R) for n in ("hi", "lo")]
        wk_s = [sb(f"wk_{n}", [128, LB, 256], F32R) for n in ("hi", "lo")]
        wv_s = [sb(f"wv_{n}", [128, LB, 256], F32R) for n in ("hi", "lo")]
        wbase_s = [sb(f"wbase_{n}", [128, LB, C], F32R) for n in ("hi", "lo")]
        wsmall_s = sb("wsmall_s", [128, LB, 136])
        lorab_s = [sb(f"lorab_{n}", [128, 1, C], F32R) for n in ("hi", "lo")]
        wall_s = sb("wall_s", [128, NSESS, HID])
        ohs = sb("ohs", [128, NSESS, NG * NU])
        ohg = sb("ohg", [128, NSESS, NU])
        seqs = sb("seqs", [128, B])
        w2bd = sb("w2bd", [128, 64])
        bsel = sb("bsel", [128, 64])
        wbd = [sb(f"wbd_{n}", [128, NU, 256], F32R) for n in ("hi", "lo")]
        y_hi = sb("y_hi", [128, LB, TOK], F32R)
        y_lo = sb("y_lo", [128, LB, TOK], F32R)
        c2T_hi = sb("c2T_hi", [128, 2, LB, 128], F32R)
        c2T_lo = sb("c2T_lo", [128, 2, LB, 128], F32R)
        q_st = sb("q_st", [128, 4, TOK])
        k_st = sb("k_st", [128, 2, TOK])
        v_st = sb("v_st", [128, NU, 2, 8 * VW])
        kbd = sb("kbd", [128, 2, 4, TOK])
        vbd = sb("vbd", [128, 2, 4, 4, 8 * VW])
        big = sb("big", [128, 16384])
        yT = big[:, :].rearrange("p (l b h) -> p l b h", l=LB, b=B)
        yG = big[:, :].rearrange("p (l g t) -> p l g t", l=LB, g=NG)
        S = big[:, 0:2048].rearrange("p (s n) -> p s n", s=2)
        ET = big[:, 2048:4096].rearrange("p (s n) -> p s n", s=2)
        x1 = big[:, 4096:6144].rearrange("p (u n) -> p u n", u=NU)
        xg = big[:, 6144:8192].rearrange("p (u n) -> p u n", u=NU)
        c2s = big[:, 8192:9216].rearrange("p (s n) -> p s n", s=2)
        hsm = big[:, 9216:9760].rearrange("p (u n) -> p u n", u=NU)
        rt = big[:, 9760:10016].rearrange("p (m n) -> p m n", m=8)
        rinv = big[:, 10016:10048].rearrange("p (f m) -> p f m", f=2)
        rmax = big[:, 10048:10112].rearrange("p (s m) -> p s m", s=2)
        bsg = big[:, 10144:10152]
        seqg = big[:, 10152:10168]
        within = big[:, 10168:10232].rearrange("p (c b) -> p c b", c=LB)
        gel = big[:, 12288:14336].rearrange("p (s q n) -> p s q n", s=2, q=2)
        def session_tiles(at):
            return [at[:, a:b].rearrange("p (u n) -> p u n", u=NU) for a, b in ((0, 256), (256, 512), (512, 1536))]
        made_in_ET = session_tiles(big[:, 2048:4096])
        made_in_q = session_tiles(q_st[:, :, :].rearrange("p a b -> p (a b)")[:, 512:2048])
        qbd = [big[:, a:a + 2048].rearrange("p (b q t) -> p b q t", b=GB, q=4) for a in (10240, 14336)]
        hw = c2s[:, 0, :].rearrange("p (u n) -> p u n", u=NU)
        hwT = [c2[:, 0, :, :] for c2 in (c2T_hi, c2T_lo)]
        pair = c2s[:, 1, :].rearrange("p (s n) -> p s n", s=2)
        x1_hi, x1_lo = ([c2[:, k, :, :].rearrange("p c n -> p (c n)") for k in range(2)] + [y[:, k, :] for k in range(2)]
                        for c2, y in ((c2T_hi, y_hi), (c2T_lo, y_lo)))
        modes = kbd[:, :, :, :].rearrange("p a b c -> p (a b c)")
        ang = vbd[:, :, :, :, :].rearrange("p a b c d -> p (a b c d)")
        L_ = big[:, 0:512]
        R_ = big[:, 512:1536]
        LR_ = big[:, 0:1536]
        zrow = big[0:32, 1536:1664]
        If = big[:, 1664:1664 + IW]
        wstage = big[:, 2048:8736]
        E_ = big[:, 8736:8736 + SW]
        I_ = big[:, 9216:9216 + IW].bitcast(I32)
        btmp = big[:, 9664:9728]
        chans = big[:, 9728:9760]
        toep = [modes[:, C * k:C * k + C] for k in range(4)]
        xs = [q_st[:, k, :] for k in range(4)]
        toep_s = [[t[:, k, :, :].rearrange("p c n -> p (c n)") for k in range(2)]
                  + [w[:, 2 * k:2 * k + 2, :].rearrange("p u n -> p (u n)") for k in range(2)]
                  for t, w in zip((c2T_hi, c2T_lo), wbd)]
        xs_s = (y_hi, y_lo)
        lmask = k_st[:, 0, :].rearrange("p (l b) -> p l b", l=LB)

        ps = [ctx.enter_context(nc.psum_tensor(f"ps{i}", [128, 512], F32)) for i in range(8)]

        def par(name, lo=0, hi=128):
            a, b = PCOL[name]
            return P_[lo:hi, a:b]

        def con(name, lo=0, hi=128):
            a, b = CCOL[name]
            return K_[lo:hi, a:b]

        def ear(name, lo=0, hi=128):
            a, b = SCOL[name]
            return E_[lo:hi, a:b]

        def num(name):
            a, b = ICOL[name]
            return If[:, a:b]

        names = """early_in params_in ints_in wsess_in w2_in weights_in wsmall_in lo_made setup dve_step w2_zero pool_step
            modes_made grown tanh_made exps_made divided angles_made sines_made coef_made basis_made
            modes_ready kern_done kern_sb kpad_in thi_made tlo_made xhi_made xlo_made conv_done
            conv_taken y_spilled y_in yhi_made ylo_made proj_done qk_taken v_taken qbd_made kbd_in
            v_stored preset v_ones scores_done scores_taken row_max shifted exp_done transposed
            attn_done rsum_inv norm_taken x_in x1_made x1hi_made x1lo_made xb_made cond_step wbd_part
            tables_made wbd_made h_done gelu_done within_made c2_done c2_biased c2_masked c2hi_made
            c2lo_made base_done small_done small_taken row_zt router_step hw_made hwT_done hwT_hi hwT_lo
            out_done out_taken""".split()
        s = {n: sem(n) for n in names}
        (early_in, params_in, ints_in, wsess_in, w2_in, weights_in, wsmall_in, lo_made, setup, dve_step, w2_zero,
         pool_step, modes_made, grown, tanh_made, exps_made, divided, angles_made, sines_made, coef_made,
         basis_made, modes_ready, kern_done, kern_sb, kpad_in, thi_made, tlo_made, xhi_made, xlo_made,
         conv_done, conv_taken, y_spilled, y_in, yhi_made, ylo_made, proj_done, qk_taken, v_taken, qbd_made,
         kbd_in, v_stored, preset, v_ones, scores_done, scores_taken, row_max, shifted, exp_done,
         transposed, attn_done, rsum_inv, norm_taken, x_in, x1_made, x1hi_made, x1lo_made, xb_made,
         cond_step, wbd_part, tables_made, wbd_made, h_done, gelu_done, within_made, c2_done, c2_biased,
         c2_masked, c2hi_made, c2lo_made, base_done, small_done, small_taken, row_zt, router_step, hw_made,
         hwT_done, hwT_hi, hwT_lo, out_done, out_taken) = [s[n] for n in names]
        hi_made = [sem(f"hi_made{n}") for n in range(5)]
        toep_in = [sem(f"toep_in{k}") for k in range(4)]
        xs_in = [sem(f"xs_in{k}") for k in range(4)]
        vbd_in = [sem(f"vbd_in{k}") for k in range(2)]
        stored = [sem(f"stored{u}") for u in range(NU)]

        NV, NU_ = 32 * KK, 32 * KI
        v0, u0, u1, end = 96, 96 + NV, 96 + NV + NU_, 96 + NV + 2 * NU_
        th = modes[:, 0:96]
        thV = modes[:, 96:96 + NV]
        thU = modes[:, 96 + NV:96 + NV + NU_]
        expV = modes[:, 1632:1632 + NV]
        expU = modes[:, 1632 + NV:1632 + NV + NU_]
        red = ang[:, 0:end]
        snb = ang[:, end:2 * end]
        tmpa = big[:, 10240:10240 + end]
        ucr = big[:, 12800:12800 + NU_]
        uci = big[:, 13312:13312 + NU_]
        tU = modes[:, 3168:4096]
        ksb = v_st[:, :, :, :].rearrange("p a b c -> p (a b c)")[:, 0:256]

        def small(n):
            return tU[:, 32 * n:32 * n + 32]

        def small2(n):
            return tU[:, 32 * n:32 * n + 64]

        def over_n(a, n):
            return a.rearrange("p (h o) -> p h o", o=1).broadcast_to([128, 32, n])

        def outer(eng, o, a, vec, n):
            return eng.tensor_tensor(o.rearrange("p (h n) -> p h n", h=32), over_n(a, n),
                                     ear(vec).rearrange("p (o n) -> p o n", o=1).broadcast_to([128, 32, n]), ALU.mult)

        def store_k(eng, quarters):
            eng.wait_ge(kern_sb, 2)
            for q in quarters:
                eng.dma_start(kpad[:, 127:127 + C].rearrange("(m q) (i k) -> q i m k", q=4, k=KK)[q],
                              ksb[32 * q:32 * q + KI, :].rearrange("i (m k) -> i m k", k=KK)).then_inc(kpad_in, 16)

        causal = con("causal").rearrange("p (o n) -> p o n", o=1).broadcast_to([128, 16, T])

        def stage_of(lo, n):
            return wstage[:, lo:lo + n].rearrange("p (l n) -> p l n", l=LB)

        weights = [(wq, stage_of(0, 2048), wq_s), (wk, stage_of(2048, 1024), wk_s), (wv, stage_of(3072, 1024), wv_s),
                   (wbase, stage_of(4096, 2048), wbase_s),
                   (lorab.rearrange("p (l n) -> p l n", l=1), wstage[:, 6144:6656].rearrange("p (l n) -> p l n", l=1),
                    lorab_s)]

        def weight_lo(eng, n):
            _w, staged, (hi, lo) = weights[n]
            eng.wait_ge(hi_made[n], 1)
            eng.tensor_tensor(lo[:, :, :], staged, hi[:, :, :].bitcast(F32), ALU.subtract).then_inc(lo_made, 1)

        def products(hi_lo_a, hi_lo_b):
            (ah, al), (bh, bl) = hi_lo_a, hi_lo_b
            return (ah, bh), (ah, bl), (al, bh)

        def chunks(j):
            if isinstance(j, int) and j == 0:
                return [("k", 0), ("k", 1), ("v", 0), ("v", 1)] + [("q", n) for n in range(4)] + [("v", 2), ("v", 3)]
            return [("q", 0), ("v", 0), ("q", 1), ("v", 1), ("q", 2), ("v", 2), ("q", 3), ("v", 3), ("k", 0), ("k", 1)]

        def taken_before(j, c, kinds):
            return sum(kind in kinds for kind, _n in chunks(j)[:c])

        def chunk_of(j, kind, n):
            return chunks(j).index((kind, n))

        block = ctx.enter_context(nc.Block())

        @block.sync
        def _(sp):
            sp.dma_start(E_[:, :], early).then_inc(early_in, 16)
            sp.dma_start(I_[:, :], ints).then_inc(ints_in, 16)
            for w, staged, _split in weights:
                sp.dma_start(staged, w).then_inc(weights_in, 16)
            sp.dma_start(K_[:, :], cst).then_inc(params_in, 16)
            sp.dma_start(P_[:, :], pk).then_inc(params_in, 16)

            def load_x(t, k):
                if not isinstance(t, int) or t > 0:
                    sp.wait_ge(xlo_made, 4 * t + k - 3)
                    sp.wait_ge(ints_in, 16)
                sp.dma_start(xs[k], xT[4 * t + k]).then_inc(xs_in[k], 16)

            for k in range(4):
                load_x(0, k)
            sp.dma_start(wsmall_s[:, :, :], wsmall).then_inc(wsmall_in, 16)
            store_k(sp, (0, 1))
            with sp.Fori(1, 8) as t:
                for k in range(4):
                    load_x(t, k)
            sp.wait_ge(conv_taken, 32)
            for g in range(2, NG):
                sp.dma_start(yspill[g], yG[:, :, g, :]).then_inc(y_spilled, 16)

            def place_k(j, waits):
                if waits:
                    wait(sp, scores_done, 8 * j)
                wait(sp, qk_taken, 6 * j + (6 if waits else 2))
                for e in range(2):
                    for r in range(4):
                        p = 64 * e + 16 * r
                        sp.dma_start(kbd[p:p + 16, :, r, :], k_st[p:p + 16, :, :]).then_inc(kbd_in, 16)

            def store_v(j):
                sp.wait_ge(v_taken, 4 * j + 4)
                sp.wait_ge(ints_in, 16)
                sp.dma_start(vrows[j].rearrange("u b k e w -> (b k) u e w"), v_st[:, :, :, :]).then_inc(v_stored, 16)

            def place_v(j, u):
                wait(sp, v_stored, 16 * j + 16)
                wait(sp, attn_done, 2 * (4 * j + u) - 2)
                sp.wait_ge(ints_in, 16)
                for ge in range(4):
                    sp.dma_start(vbd[32 * ge:32 * ge + 32, u % 2, :, ge, :],
                                 vrows[j, u, :, :, ge % 2, :].rearrange("b k w -> k b w")).then_inc(vbd_in[u % 2], 16)

            def load_y(j):
                wait(sp, h_done, 8 * (j - 1))
                sp.wait_ge(y_spilled, 16 * (NG - 2))
                sp.dma_start(y_lo[:, :, :].bitcast(F32), yspill[j]).then_inc(y_in, 16)

            sp.wait_ge(preset, 2)
            place_k(0, False)
            store_v(0)
            place_v(0, 0); place_v(0, 1)
            sp.wait_ge(y_spilled, 16 * (NG - 2))
            for u in range(NU):
                sp.dma_start(xg[:, u, :], xN[0, :, u, :]).then_inc(x_in, 16)

            def group(i, more_y, more):
                place_v(i, 2); place_v(i, 3)
                if more:
                    place_k(i + 1, True)
                    store_v(i + 1)
                    place_v(i + 1, 0); place_v(i + 1, 1)
                if more_y:
                    load_y(i + 2)
                for u in range(NU):
                    sp.wait_ge(out_taken, 4 * i + u + 1)
                    sp.wait_ge(ints_in, 16)
                    sp.dma_start(out[i, :, u, :], xg[:, u, :]).then_inc(stored[u], 16)
                if more:
                    for u in range(NU):
                        sp.wait_ge(stored[u], 16 * i + 16)
                        sp.wait_ge(ints_in, 16)
                        sp.dma_start(xg[:, u, :], xN[i + 1, :, u, :]).then_inc(x_in, 16)

            group(0, True, True)
            with sp.Fori(1, 6) as i:
                group(i, True, True)
            group(6, False, True)
            group(7, False, False)
            for u in range(NU):
                sp.wait_ge(stored[u], 16 * NG)

        @block.tensor
        def _(pe):
            pe.wait_ge(basis_made, 1)
            pe.wait_ge(modes_ready, 1)
            for h in range(32):
                q, m = h % 4, h // 4
                mm = pe.matmul(ps[6][32 * q:32 * q + 32, m * KK:(m + 1) * KK], LR_[:, h * KI:h * KI + 32],
                               R_[:, h * KK:(h + 1) * KK], start=True, stop=True)
            mm.then_inc(kern_done, 1)

            def conv(t, k):
                pe.wait_ge(tlo_made, 4 * t + k + 1)
                pe.wait_ge(xlo_made, 4 * t + k + 1)
                if not isinstance(t, int) or t > 0:
                    pe.wait_ge(conv_taken, 4 * t + k - 3)
                for d in range(LB):
                    for m, (a, x) in enumerate(products(toep_s, xs_s)):
                        mm = pe.matmul(ps[k][:, 128 * d:512], a[k][:, 128 * d:128 * d + 128],
                                       x[:, k, 0:512 - 128 * d], start=(d == 0 and m == 0),
                                       stop=(d == LB - 1 and m == 2))
                mm.then_inc(conv_done, 1)

            for k in range(4):
                conv(0, k)
            with pe.Fori(1, 8) as t:
                for k in range(4):
                    conv(t, k)

            def project(j, c):
                kind, n = chunks(j)[c]
                bank = ps[4 + c % 2]
                if c == 0:
                    wait(pe, v_taken, 4 * j)
                    wait(pe, small_taken, 4 * (j - 1))
                    wait(pe, hwT_lo, j - 1)
                elif c >= 2:
                    if chunks(j)[c - 2][0] == "v":
                        pe.wait_ge(v_taken, 4 * j + taken_before(j, c - 1, "v"))
                    else:
                        pe.wait_ge(qk_taken, 6 * j + taken_before(j, c - 1, "qk"))
                a = 128 * n
                for l in range(LB):
                    if c == 0:
                        pe.wait_ge(yhi_made, LB * j + l + 1)
                    for m, (y, w) in enumerate(products((y_hi, y_lo), {"q": wq_s, "k": wk_s, "v": wv_s}[kind])):
                        if c == 0 and m == 2:
                            pe.wait_ge(ylo_made, LB * j + l + 1)
                        f = dict(start=(l == 0 and m == 0), stop=(l == LB - 1 and m == 2))
                        if kind == "v":
                            mm = pe.matmul(bank[:, 0:256], y[:, l, a:a + 128], w[:, l, :], **f)
                        else:
                            mm = pe.matmul(bank[:, :], w[:, l, a:a + 128], y[:, l, :], **f)
                mm.then_inc(proj_done, 1)

            def scores(i, u):
                n = 4 * i + u
                if u == 0:
                    pe.wait_ge(qbd_made, 8 * i + 8)
                    pe.wait_ge(kbd_in, 16 * 8 * (i + 1))
                    wait(pe, c2_biased, 4 * i)
                for k in range(2):
                    wait(pe, scores_taken, 2 * n + k - 1)
                    for b in (4 * u + 2 * k, 4 * u + 2 * k + 1):
                        for f in range(2):
                            at = 256 * (b % 2) + 128 * f
                            mm = pe.matmul(ps[k][:, at:at + 128], qbd[f][:, b, :, :],
                                           kbd[:, f, :, 32 * b:32 * b + 32], start=True, stop=True)
                    mm.then_inc(scores_done, 1)

            def scores_and_mask(i, u):
                n = 4 * i + u
                for k in range(2):
                    bank = ps[4 * (u % 2) + k]
                    if u == 1:
                        pe.wait_ge(small_taken, 4 * i)
                        pe.wait_ge(hwT_lo, i)
                    else:
                        pe.wait_ge(scores_taken, 2 * n + k - 3)
                    pe.matmul(bank[:, :], con("ident"), causal, start=True, stop=False)
                    for b in (4 * u + 2 * k, 4 * u + 2 * k + 1):
                        for f in range(2):
                            at = 256 * (b % 2) + 128 * f
                            mm = pe.matmul(bank[:, at:at + 128], qbd[f][:, b, :, :],
                                           kbd[:, f, :, 32 * b:32 * b + 32], start=False,
                                           stop=(b % 2 == 1 and f == 1))
                    mm.then_inc(scores_done, 1)

            def attend(i, u):
                n = 4 * i + u
                pe.wait_ge(vbd_in[u % 2], 16 * 4 * (2 * i + u // 2 + 1))
                if u == 0:
                    wait(pe, out_taken, 4 * i - 2)
                pe.wait_ge(transposed, n + 1)
                for f in range(2):
                    wait(pe, norm_taken, 2 * n + f - 1)
                    for r in range(4):
                        for b in range(4):
                            at = 256 * b + 128 * f + 32 * r
                            v = (4 * f + r) * VW
                            mm = pe.matmul(ps[2 + f][32 * b:32 * b + 32, 68 * r:68 * r + 68],
                                           ET[:, u % 2, at:at + 32], vbd[:, u % 2, b, :, v:v + VW],
                                           start=True, stop=True)
                    mm.then_inc(attn_done, 1)

            def cond_h(i, u):
                n = 4 * i + u
                pe.wait_ge(x1lo_made, n + 1)
                if u == 0:
                    pe.wait_ge(wbd_made, 4 * i + 4)
                    wait(pe, out_taken, 4 * i)
                for p in range(2):
                    wait(pe, gelu_done, 2 * n + p - 1)
                    for m, (w, x) in enumerate(products(wbd, (x1_hi[u], x1_lo[u]))):
                        mm = pe.matmul(ps[6 + p][:, :], w[:, u, 128 * p:128 * p + 128], x,
                                       start=(m == 0), stop=(m == 2))
                    mm.then_inc(h_done, 1)

            def cond_out(i, u):
                n = 4 * i + u
                pe.wait_ge(gelu_done, 2 * n + 2)
                if u == 0:
                    pe.wait_ge(scores_taken, 8 * i + 8)
                wait(pe, c2_biased, n - 1)
                for c in range(LB):
                    for p in range(2):
                        mm = pe.matmul(ps[u % 2][:, 128 * c + 64 * p:128 * c + 64 * p + 64],
                                       gel[:, u % 2, p, 128 * c:128 * c + 128], w2bd[:, :], start=True, stop=True)
                mm.then_inc(c2_done, 1)

            def router_lora(i, u, last):
                n = 4 * i + u
                pe.wait_ge(c2_masked, n + 1)
                if u < 2:
                    pe.wait_ge(qk_taken, 6 * i + (6 if last else 12))
                else:
                    pe.wait_ge(small_taken, n - 1)
                for c in range(LB):
                    mm = pe.matmul(ps[4 + u % 2][:, 0:136], c2s[:, u % 2, 128 * c:128 * c + 128], wsmall_s[:, c, :],
                                   start=(c == 0), stop=(c == LB - 1))
                mm.then_inc(small_done, 1)

            out_bank = [ps[2], ps[3], ps[6], ps[7]]

            def base(i, u):
                if u == 0:
                    pe.wait_ge(norm_taken, 8 * i + 8)
                if u == 2:
                    pe.wait_ge(gelu_done, 8 * i + 8)
                pe.wait_ge(c2lo_made, 4 * i + u + 1)
                for c in range(LB):
                    for m, (a, w) in enumerate(products((c2T_hi, c2T_lo), wbase_s)):
                        mm = pe.matmul(out_bank[u][:, :], a[:, u % 2, c, :], w[:, c, :],
                                       start=(c == 0 and m == 0), stop=False)
                mm.then_inc(base_done, 1)

            def turn_h(i):
                pe.wait_ge(hw_made, i + 1)
                pe.wait_ge(small_taken, 4 * i + 4)
                for u in range(NU):
                    mm = pe.transpose(ps[4][:, 128 * u:128 * u + 128], hw[:, u, :], con("ident"))
                mm.then_inc(hwT_done, 1)

            def expert(i, u):
                if u == 0:
                    pe.wait_ge(hwT_hi, i + 1)
                for m, (a, w) in enumerate(products(hwT, lorab_s)):
                    if u == 0 and m == 2:
                        pe.wait_ge(hwT_lo, i + 1)
                    mm = pe.matmul(out_bank[u][:, :], a[:, u, :], w[:, 0, :], start=False, stop=(m == 2))
                mm.then_inc(out_done, 1)

            def group(i, last=False):
                def A(c):
                    if not last:
                        project(i + 1, c)
                if last:
                    scores_and_mask(i, 1); scores_and_mask(i, 2); attend(i, 0)
                    scores_and_mask(i, 3); attend(i, 1); attend(i, 2); cond_h(i, 0)
                else:
                    A(0)
                    scores(i, 1); A(1); attend(i, 0); A(2)
                    scores(i, 2); A(3); attend(i, 1); A(4)
                    scores(i, 3); A(5); attend(i, 2); A(6); A(7); A(8); A(9); cond_h(i, 0)
                attend(i, 3)
                for k in range(NU + 3):
                    if 1 <= k < NU:
                        cond_h(i, k)
                    if 1 <= k <= NU:
                        cond_out(i, k - 1)
                    if k >= 3:
                        router_lora(i, k - 3, last)
                        if k < NU + 1:
                            base(i, k - 3)
                base(i, 2); base(i, 3)
                turn_h(i)
                if not last:
                    scores(i + 1, 0)
                for u in range(NU):
                    expert(i, u)

            pe.wait_ge(lo_made, len(weights))
            for c in range(10):
                project(0, c)
            pe.wait_ge(w2_in, 32)
            pe.wait_ge(wsmall_in, 16)
            pe.wait_ge(params_in, 32)
            scores(0, 0)
            group(0)
            with pe.Fori(1, 7) as i:
                group(i)
            group(7, last=True)

        @block.scalar
        def _(act):
            for q in range(4):
                act.dma_start(wall_s[32 * q:32 * q + 32, :, :], wsess).then_inc(wsess_in, 16)
            act.wait_ge(w2_zero, 1)
            for p in range(2):
                act.dma_start(w2bd[64 * p:64 * p + 64, 32 * p:32 * p + 32], w2).then_inc(w2_in, 16)
            act.wait_ge(kern_sb, 1)
            act.dma_start(kpad[:, 0:127], zrow[:, 0:127]).then_inc(kpad_in, 16)

            def weight_hi(n):
                act.wait_ge(weights_in, 16 * len(weights))
                act.activation(weights[n][2][0][:, :, :], weights[n][1], ACT.Copy).then_inc(hi_made[n], 1)

            act.wait_ge(modes_made, 1)
            act.activation(small(6), small(5), ACT.Tanh, scale=0.5).then_inc(tanh_made, 1)
            act.wait_ge(grown, 2)
            act.activation(expV, expV, ACT.Exp).then_inc(exps_made, 1)
            act.activation(expU, expU, ACT.Exp).then_inc(exps_made, 1)
            act.wait_ge(angles_made, 1)
            act.activation(snb[:, 0:v0], red[:, 0:v0], ACT.Sin).then_inc(sines_made, 1)
            weight_hi(1)
            act.wait_ge(angles_made, 2)
            act.activation(snb[:, v0:u0], red[:, v0:u0], ACT.Sin, bias=ear("angle")[:, 0:1]).then_inc(sines_made, 1)
            weight_hi(2)
            weight_hi(4)
            act.wait_ge(angles_made, 3)
            act.activation(snb[:, u0:u1], red[:, u0:u1], ACT.Sin, bias=ear("angle")[:, 1:2]).then_inc(sines_made, 1)
            act.activation(snb[:, u1:end], red[:, u1:end], ACT.Sin, bias=ear("angle")[:, 2:3]).then_inc(sines_made, 1)
            weight_hi(0)
            def x_high(t, k, first=False):
                h = 4 * t + k
                act.wait_ge(xs_in[k], 16 * t + 16)
                if not first:
                    act.wait_ge(conv_done, h - 3)
                act.activation(xs_s[0][:, k, :], xs[k], ACT.Copy).then_inc(xhi_made, 1)

            for k in range(4):
                x_high(0, k, first=True)
            store_k(act, (2, 3))
            weight_hi(3)
            act.wait_ge(kpad_in, 16 * 5)

            def load_toep(t, k, first=False):
                if not first:
                    act.wait_ge(tlo_made, 4 * t + k - 3)
                    act.wait_ge(kpad_in, 16 * 5)
                rows = bass.AP(kpad.tensor, (4 * t + k) * PADW + kpad.offset, [[1, 128], [1, C]])
                act.dma_start(toep[k], rows).then_inc(toep_in[k], 16)

            def conv_hi(t, k, more_x=True, more_k=True):
                h = 4 * t + k
                wait(act, conv_done, h - 3)
                act.wait_ge(toep_in[k], 16 * t + 16)
                act.activation(toep_s[0][k], toep[k], ACT.Copy).then_inc(thi_made, 1)
                if more_x:
                    x_high(*((t, k + 1) if k < 3 else (t + 1, 0)))
                if more_k:
                    load_toep(*((t, 3) if k == 0 else (t + 1, k - 1)))

            for k in range(4):
                load_toep(0, k, first=True)
            for k in range(4):
                conv_hi(0, k, more_x=k == 3, more_k=k > 0)
            with act.Fori(1, 7) as t:
                for k in range(4):
                    conv_hi(t, k)
            for k in range(4):
                conv_hi(7, k, more_x=k < 3, more_k=k == 0)

            def take(j, c):
                kind, n = chunks(j)[c]
                act.wait_ge(proj_done, 10 * j + c + 1)
                if (kind, n) == ("q", 0):
                    wait(act, qbd_made, 8 * j)
                if (kind, n) == ("q", 1) and isinstance(j, int) and j == 0:
                    act.wait_ge(wbd_part, 2 * NU)
                if (kind, n) == ("q", 2) and isinstance(j, int) and j == 0:
                    act.wait_ge(wbd_made, NU)
                if (kind, n) == ("k", 0):
                    wait(act, kbd_in, 16 * 8 * j)
                staging, bias = (q_st, par("bq")) if kind == "q" else (k_st, par("bk"))
                act.activation(staging[:, n, :], ps[4 + c % 2][:, :], ACT.Identity,
                               bias=bias[:, n:n + 1]).then_inc(qk_taken, 1)

            def expo(i, u, last):
                n = 4 * i + u
                if last and u:
                    act.wait_ge(scores_taken, 2 * n + 2)
                else:
                    act.wait_ge(shifted, n + 1)
                act.activation(S[:, u % 2, :], S[:, u % 2, :], ACT.Exp, scale=SCALE).then_inc(exp_done, 1)

            def gelu(i, u, p):
                n = 4 * i + u
                wait(act, c2_done, n - 1)
                act.wait_ge(h_done, 2 * n + p + 1)
                act.activation(gel[:, u % 2, p, :], ps[6 + p][:, :], ACT.Gelu,
                               bias=bsg[:, 2 * u + p:2 * u + p + 1]).then_inc(gelu_done, 1)

            def x1_high(i, u, last):
                n = 4 * i + u
                if u < 2:
                    wait(act, out_done, 4 * i)
                else:
                    act.wait_ge(proj_done, 10 * i + (10 if last else 20))
                act.wait_ge(x1_made, n + 1)
                act.activation(x1_hi[u], x1[:, u, :], ACT.Copy).then_inc(x1hi_made, 1)

            def c2_high(i, u):
                n = 4 * i + u
                wait(act, base_done, n - 1)
                act.wait_ge(c2_masked, n + 1)
                act.activation(c2T_hi[:, u % 2, :, :], c2s[:, u % 2, :].rearrange("p (c n) -> p c n", c=LB),
                               ACT.Copy).then_inc(c2hi_made, 1)

            def take_small(i, u):
                act.wait_ge(small_done, 4 * i + u + 1)
                wait(act, hw_made, i)
                act.activation(hsm[:, u, :], ps[4 + u % 2][:, 0:136], ACT.Copy).then_inc(small_taken, 1)

            def take_hw(i):
                act.wait_ge(base_done, 4 * i + 3)
                act.wait_ge(hwT_done, i + 1)
                act.activation(hwT[0], ps[4][:, :].rearrange("p (u n) -> p u n", u=NU), ACT.Copy).then_inc(hwT_hi, 1)

            def group(i, more_y=True, last=False):
                def A(c):
                    if not last:
                        take(i + 1, c)
                expo(i, 0, last); A(0)
                expo(i, 1, last); A(2)
                expo(i, 2, last); A(4); x1_high(i, 0, last)
                expo(i, 3, last); x1_high(i, 1, last)
                A(6); A(8); A(9)
                x1_high(i, 2, last)
                for k in range(NU + 3):
                    if k < NU:
                        gelu(i, k, 0); gelu(i, k, 1)
                    if k == 0:
                        x1_high(i, NU - 1, last)
                    if 2 <= k <= NU + 1:
                        c2_high(i, k - 2)
                    if k >= 3:
                        take_small(i, k - 3)
                if more_y:
                    split_hi(i + 2)
                take_hw(i)

            def split_hi(j):
                here = isinstance(j, int) and j < 2
                if here:
                    wait(act, proj_done, 10 * j)
                else:
                    act.wait_ge(y_in, 16 * (j - 1))
                for l in range(LB):
                    src = yG[:, l, j, :] if here else y_lo[:, l, :].bitcast(F32)
                    act.activation(y_hi[:, l, :], src, ACT.Copy).then_inc(yhi_made, 1)

            act.wait_ge(conv_taken, 32)
            split_hi(0)
            act.wait_ge(params_in, 32)
            for c, (kind, _n) in enumerate(chunks(0)):
                if kind != "v":
                    take(0, c)
            split_hi(1)
            group(0)
            with act.Fori(1, 6) as i:
                group(i)
            group(6, more_y=False)
            group(7, more_y=False, last=True)

        @block.gpsimd
        def _(pool):
            steps = [0]

            def step(ins):
                steps[0] += 1
                ins.then_inc(pool_step, 1)
                pool.wait_ge(pool_step, steps[0])

            pool.memset(w2bd[:, :], 0.0).then_inc(w2_zero, 1)
            pool.wait_ge(modes_made, 1)
            outer(pool, expV, small(5), "kvec", KK).then_inc(grown, 1)
            outer(pool, expU, small(5), "ivec", KI).then_inc(grown, 1)
            def mul(o, a, b, op=ALU.mult):
                step(pool.tensor_tensor(o, a, b, op))

            em, er, ei, t0, t1, nr, ni = small(0), small(1), small(7), small(10), small(11), small(12), small(13)
            am, ai, cre, cim = small(9), ear("aimag"), ear("cre"), ear("cim")
            sn, cs, sh = snb[:, 0:32], snb[:, 32:64], snb[:, 64:96]
            pool.wait_ge(divided, 1)
            pool.wait_ge(sines_made, 1)
            step(pool.tensor_scalar(t0, em, 1.0, 1.0, ALU.add, ALU.mult))
            mul(ei, t0, sn)
            mul(er, em, cs)
            mul(t0, sh, sh)
            step(pool.tensor_scalar(t0, t0, -2.0, 0.0, ALU.mult, ALU.add))
            mul(er, er, t0, ALU.add)
            mul(nr, cre, er)
            mul(t0, cim, ei)
            mul(nr, nr, t0, ALU.subtract)
            mul(ni, cre, ei)
            mul(t0, cim, er)
            mul(ni, ni, t0, ALU.add)
            mul(t0, nr, am)
            mul(t1, ni, ai)
            mul(t0, t1, t0, ALU.subtract)
            mul(t1, nr, ai)
            mul(nr, ni, am)
            mul(t1, t1, nr, ALU.add)
            mul(t0, t0, small(2))
            mul(t1, t1, small(3))
            pool.wait_ge(exps_made, 2)
            eU = expU.rearrange("p (h n) -> p h n", h=32)
            pool.tensor_tensor(ucr.rearrange("p (h n) -> p h n", h=32), eU, over_n(t0, KI), ALU.mult).then_inc(coef_made, 1)
            pool.tensor_tensor(uci.rearrange("p (h n) -> p h n", h=32), eU, over_n(t1, KI), ALU.mult).then_inc(coef_made, 1)
            pool.wait_ge(sines_made, 2)
            pool.tensor_tensor(R_, expV, snb[:, v0:u0], ALU.mult).then_inc(basis_made, 1)
            for n in (1, 2, 4):
                weight_lo(pool, n)
            pool.wait_ge(basis_made, 1)
            pool.wait_ge(modes_ready, 1)
            pool.memset(vbd[:, :, :, :, :], 0.0).then_inc(preset, 1)
            def conv_lo(t, k):
                h = 4 * t + k
                wait(pool, conv_done, h - 3)
                pool.wait_ge(thi_made, h + 1)
                pool.tensor_tensor(toep_s[1][k], toep[k], toep_s[0][k].bitcast(F32),
                                   ALU.subtract).then_inc(tlo_made, 1)

            for k in range(4):
                conv_lo(0, k)
            with pool.Fori(1, 8) as t:
                for k in range(4):
                    conv_lo(t, k)
            def split_lo(j):
                for l in range(LB):
                    pool.wait_ge(yhi_made, LB * j + l + 1)
                    pool.tensor_tensor(y_lo[:, l, :], y_lo[:, l, :].bitcast(F32), y_hi[:, l, :].bitcast(F32),
                                       ALU.subtract).then_inc(ylo_made, 1)

            def residual(i, u):
                n = 4 * i + u
                if u == 0:
                    pool.wait_ge(x_in, 64 * i + 64)
                pool.wait_ge(norm_taken, 2 * n + 2)
                pool.tensor_tensor(x1[:, u, :], x1[:, u, :], xg[:, u, :], ALU.add).then_inc(x1_made, 1)
                pool.wait_ge(x1_made, n + 1)
                pool.tensor_tensor(xg[:, u, :], x1[:, u, :], par("bbase"), ALU.add).then_inc(xb_made, 1)

            NSTEP = 2 * NSESS

            def conditions(i):
                wacc, wtmp, wdiag = made_in_q if isinstance(i, int) and i == 0 else made_in_ET
                k = [0]
                wait(pool, h_done, 8 * i)

                def then(ins):
                    k[0] += 1
                    ins.then_inc(cond_step, 1)
                    pool.wait_ge(cond_step, NSTEP * i + k[0])

                then(pool.tensor_copy(ohg[:, :, :], ohs[:, :, bass.ds(4 * i, 4)]))
                for m in range(NSESS):
                    then(pool.tensor_tensor(wtmp if m else wacc, wall_s[:, m:m + 1, :].broadcast_to([128, NU, HID]),
                                            ohg[:, m, :].rearrange("p (u o) -> p u o", o=1).broadcast_to([128, NU, HID]),
                                            ALU.mult))
                    if m:
                        then(pool.tensor_tensor(wacc, wacc, wtmp, ALU.add))
                assert k[0] == NSTEP
                own = con("own").rearrange("p (b o) -> p b o", o=1).broadcast_to([128, 4, HID])
                for u in range(NU):
                    w = wacc[:, u:u + 1, :].broadcast_to([128, 4, HID])
                    pool.tensor_tensor(wbd[0][:, u, :].rearrange("p (b n) -> p b n", b=4), w, own, ALU.mult).then_inc(wbd_part, 1)
                    pool.tensor_tensor(wdiag[:, u, :].rearrange("p (b n) -> p b n", b=4), w, own, ALU.mult).then_inc(wbd_part, 1)
                for u in range(NU):
                    pool.wait_ge(wbd_part, 8 * i + 2 * u + 2)
                    pool.tensor_tensor(wbd[1][:, u, :], wdiag[:, u, :], wbd[0][:, u, :].bitcast(F32),
                                       ALU.subtract).then_inc(wbd_made, 1)

            def tables(i):
                pool.tensor_copy(bsg[:, :], bsel[:, bass.ds(8 * i, 8)]).then_inc(tables_made, 1)
                pool.tensor_copy(seqg[:, :], seqs[:, bass.ds(GB * i, GB)]).then_inc(tables_made, 1)

            def group(i, more_y=False, last=False):
                residual(i, 0)
                tables(i)
                for u in range(1, NU):
                    residual(i, u)
                if not last:
                    conditions(i + 1)
                if more_y:
                    split_lo(i + 2)

            pool.wait_ge(setup, NSESS + 1)
            pool.wait_ge(wsess_in, 64)
            pool.wait_ge(params_in, 32)
            pool.wait_ge(conv_taken, 32)
            conditions(0)
            group(0, True)
            with pool.Fori(1, 6) as i:
                group(i, True)
            group(6)
            group(7, last=True)

        @block.vector
        def _(dve):
            steps = [0]

            def step(ins):
                steps[0] += 1
                ins.then_inc(dve_step, 1)
                dve.wait_ge(dve_step, steps[0])

            def tt(o, a, b, op):
                step(dve.tensor_tensor(o, a, b, op))

            def ts(o, a, s1, op0, s2=None, op1=None):
                if s2 is None:
                    step(dve.tensor_scalar(o, a, s1, None, op0))
                else:
                    step(dve.tensor_scalar(o, a, s1, s2, op0, op1))

            def stt(o, a, sc, b, op0, op1):
                step(dve.scalar_tensor_tensor(out=o, in0=a, scalar=sc, in1=b, op0=op0, op1=op1))

            dve.wait_ge(early_in, 16)
            dve.memset(zrow, 0.0).then_inc(kern_sb, 1)
            X, N_, R, PL = ear("logs"), small2(0), small2(2), small2(8)
            ts(N_, X, LOG2E, ALU.mult, MAGIC, ALU.add)
            ts(N_, N_, MAGIC, ALU.subtract)
            stt(R, N_, -LN2_HI, X, ALU.mult, ALU.add)
            stt(R, N_, -LN2_LO, R, ALU.mult, ALU.add)
            ts(PL, R, 1.0 / 5040, ALU.mult)
            for c in (1.0 / 720, 1.0 / 120, 1.0 / 24, 1.0 / 6, 0.5, 1.0):
                stt(PL, PL, c, R, ALU.add, ALU.mult)
            ts(PL, PL, 1.0, ALU.add)
            ts(N_, N_, 127.0, ALU.add, 8388608.0, ALU.mult)
            step(dve.tensor_copy(R.bitcast(I32), N_))
            tt(PL, PL, R, ALU.mult)
            dt, am = small(8), small(9)
            dr = small(5)
            stt(dr, am, -1.0, dt, ALU.mult, ALU.mult)
            dve.tensor_tensor(th[:, 0:32], ear("aimag"), dt, ALU.mult).then_inc(modes_made, 1)
            dve.wait_ge(modes_made, 1)
            ts(th[:, 32:64], th[:, 0:32], 1.0, ALU.mult)
            ts(th[:, 64:96], th[:, 0:32], 0.5, ALU.mult)
            turn, upper, lower = ear("turn"), ear("upper"), ear("lower")

            def full_turns(lo, hi, parts):
                for a, q, b, e in parts:
                    ts(tmpa[:, b:e], a, INV2PI, ALU.mult, q, ALU.add)
                ts(tmpa[:, lo:hi], tmpa[:, lo:hi], MAGIC, ALU.add, MAGIC, ALU.subtract)
                for a, _q, b, e in parts:
                    stt(red[:, b:e], tmpa[:, b:e], -TP1, a, ALU.mult, ALU.add)
                stt(red[:, lo:hi], tmpa[:, lo:hi], -TP2, red[:, lo:hi], ALU.mult, ALU.add)

            full_turns(0, 96, [(th[:, 0:32], 0.0, 0, 32), (th[:, 32:64], 0.25, 32, 64), (th[:, 64:96], 0.0, 64, 96)])
            ts(red[:, 32:64], red[:, 32:64], float(np.pi / 2), ALU.add)
            dve.tensor_scalar(red[:, 0:96], red[:, 0:96], PI_LO, -PI_LO, ALU.min, ALU.max).then_inc(angles_made, 1)
            ai, tn, em, den, t0 = ear("aimag"), small(6), small(0), small(3), small(7)
            tt(t0, am, am, ALU.mult)
            tt(den, ai, ai, ALU.mult)
            tt(den, den, t0, ALU.add)
            step(dve.reciprocal(den, den))
            ts(small(2), den, 2.0, ALU.mult)
            ts(small(3), den, -2.0, ALU.mult)
            dve.wait_ge(tanh_made, 1)
            ts(t0, tn, -1.0, ALU.mult, 1.0, ALU.add)
            step(dve.reciprocal(t0, t0))
            dve.scalar_tensor_tensor(out=em, in0=tn, scalar=2.0, in1=t0, op0=ALU.mult, op1=ALU.mult).then_inc(divided, 1)

            def bounded(n, b, e):
                return dve.tensor_scalar(red[:, b:e], red[:, b:e], upper[:, n:n + 1], lower[:, n:n + 1], ALU.min, ALU.max)

            step(outer(dve, thV, th[:, 0:32], "kvec", KK))
            full_turns(v0, u0, [(thV, turn[:, 0:1], v0, u0)])
            bounded(0, v0, u0).then_inc(angles_made, 1)
            step(outer(dve, thU, th[:, 0:32], "ivec", KI))
            full_turns(u0, end, [(thU, turn[:, 1:2], u0, u1), (thU, turn[:, 2:3], u1, end)])
            step(bounded(1, u0, u1))
            bounded(2, u1, end).then_inc(angles_made, 1)
            dve.wait_ge(sines_made, 3)
            dve.wait_ge(coef_made, 2)
            tt(L_, ucr, snb[:, u0:u1], ALU.mult)
            dve.wait_ge(sines_made, 4)
            tt(tmpa[:, 0:NU_], uci, snb[:, u1:end], ALU.mult)
            dve.tensor_tensor(L_, L_, tmpa[:, 0:NU_], ALU.add).then_inc(modes_ready, 1)
            dve.wait_ge(kern_done, 1)
            step(dve.tensor_copy(ksb, ps[6][:, 0:256]))
            k0 = ksb.rearrange("p (m k) -> p m k", k=KK)[:, :, 0]
            dve.tensor_tensor(k0, k0, ear("dskip"), ALU.add).then_inc(kern_sb, 1)

            dve.wait_ge(ints_in, 16)
            step(dve.tensor_copy(If[:, :], I_[:, :]))
            for l in range(LB):
                ts(lmask[:, l, :], num("length"), ear("lpos")[:, l:l + 1], ALU.is_gt)

            def x_lo(t, k, first=False):
                h = 4 * t + k
                if not first:
                    dve.wait_ge(conv_done, h - 3)
                dve.wait_ge(xhi_made, h + 1)
                dve.tensor_tensor(xs_s[1][:, k, :], xs[k], xs_s[0][:, k, :].bitcast(F32), ALU.subtract).then_inc(xlo_made, 1)

            x_lo(0, 0, first=True)
            x_lo(0, 1, first=True)
            weight_lo(dve, 0)
            x_lo(0, 2, first=True)
            x_lo(0, 3, first=True)
            weight_lo(dve, 3)
            cm = chans
            ts(cm, num("chans"), ear("cpos"), ALU.is_gt)
            for k in range(NSESS):
                dve.scalar_tensor_tensor(out=ohs[:, k, :], in0=num("sid_bc"), scalar=float(k), in1=cm,
                                         op0=ALU.is_equal, op1=ALU.mult).then_inc(setup, 1)
            bs = ear("bsess")
            for k in range(NSESS):
                dst = bsel[:, :] if k == 0 else btmp
                ts(dst, num("sid_ph"), float(k), ALU.is_equal, bs[:, k:k + 1], ALU.mult)
                if k:
                    tt(bsel[:, :], bsel[:, :], btmp, ALU.add)
            dve.tensor_copy(seqs[:, :], num("seq")).then_inc(setup, 1)

            def take_conv(t, k):
                dve.wait_ge(conv_done, 4 * t + k + 1)
                h = 4 * t + k
                o = yT[:, :, :, h] if isinstance(t, int) else yT[:, :, :, bass.ds(h, 1)].rearrange("p l b o -> p l (b o)")
                dve.tensor_tensor(o, ps[k][:, :].rearrange("p (l b) -> p l b", l=LB), lmask[:, :, :],
                                  ALU.mult).then_inc(conv_taken, 1)

            dve.wait_ge(setup, NSESS + 1)
            dve.wait_ge(lo_made, len(weights))
            def conv_step(t, k, ahead=True):
                if ahead:
                    x_lo(*((t, 3) if k == 0 else (t + 1, k - 1)))
                take_conv(t, k)

            for k in range(4):
                conv_step(0, k, ahead=k > 0)
            with dve.Fori(1, 7) as t:
                for k in range(4):
                    conv_step(t, k)
            for k in range(4):
                conv_step(7, k, ahead=k == 0)


            def take_v(j, u):
                c = chunk_of(j, "v", u)
                dve.wait_ge(proj_done, 10 * j + c + 1)
                if u == 0:
                    wait(dve, v_stored, 16 * j)
                dve.tensor_tensor(v_st[:, u, :, :].rearrange("p e (k w) -> p (e k) w", w=VW)[:, :, 0:16],
                                  ps[4 + c % 2][:, 0:256].rearrange("p (k w) -> p k w", w=16),
                                  par("bv").rearrange("p (k w) -> p k w", w=16), ALU.add).then_inc(v_taken, 1)

            def spread_q(j, waits, halves=(0, 1)):
                if waits:
                    wait(dve, scores_done, 8 * j)
                else:
                    dve.wait_ge(y_spilled, 16 * (NG - 2))
                for g in halves:
                    wait(dve, qk_taken, 6 * j + (4 if waits else 4 + 2 * g))
                    for f in range(2):
                        for e in range(2):
                            dve.tensor_scalar(qbd[f][:, :, 2 * g + e, :],
                                              q_st[:, 2 * g + f, :].rearrange("p (b t) -> p b t", b=GB),
                                              con("evenodd")[:, e:e + 1], None, ALU.mult).then_inc(qbd_made, 1)

            def soft(i, u):
                n = 4 * i + u
                Su = S[:, u % 2, :]
                for k in range(2):
                    dve.wait_ge(scores_done, 2 * n + k + 1)
                    dve.tensor_tensor(Su[:, 512 * k:512 * k + 512].rearrange("p (m n) -> p m n", n=T),
                                      ps[k][:, :].rearrange("p (m n) -> p m n", n=T), causal,
                                      ALU.add).then_inc(scores_taken, 1)
                dve.wait_ge(scores_taken, 2 * n + 2)
                S3 = Su.rearrange("p (m n) -> p m n", n=T)
                dve.tensor_reduce(rmax[:, u % 2, :], S3, AX, ALU.max).then_inc(row_max, 1)
                dve.wait_ge(row_max, n + 1)
                dve.tensor_tensor(S3, S3, rmax[:, u % 2, :].rearrange("p (m o) -> p m o", o=1).broadcast_to([128, 32, T]),
                                  ALU.subtract).then_inc(shifted, 1)

            def soft_masked(i, u):
                n = 4 * i + u
                wait(dve, transposed, n - 1)
                for k in range(2):
                    dve.wait_ge(scores_done, 2 * n + k + 1)
                    ins = dve.tensor_reduce(rmax[:, u % 2, 16 * k:16 * k + 16],
                                            ps[4 * (u % 2) + k][:, :].rearrange("p (m n) -> p m n", n=T), AX, ALU.max)
                ins.then_inc(row_max, 1)
                dve.wait_ge(row_max, n + 1)
                for k in range(2):
                    top = rmax[:, u % 2, 16 * k:16 * k + 16].rearrange("p (m o) -> p m o", o=1).broadcast_to([128, 16, T])
                    dve.tensor_tensor(S[:, u % 2, 512 * k:512 * k + 512].rearrange("p (m n) -> p m n", n=T),
                                      ps[4 * (u % 2) + k][:, :].rearrange("p (m n) -> p m n", n=T), top,
                                      ALU.subtract).then_inc(scores_taken, 1)

            def turn_p(i, u):
                n = 4 * i + u
                dve.wait_ge(exp_done, n + 1)
                wait(dve, attn_done, 2 * n - 2)
                if u < 2:
                    wait(dve, wbd_made, 4 * i + 4)
                dve.transpose(ET[:, u % 2, :], S[:, u % 2, :]).then_inc(transposed, 1)

            def normalise(i, u):
                n = 4 * i + u
                for f in range(2):
                    dve.wait_ge(attn_done, 2 * n + f + 1)
                    pv = ps[2 + f][:, 0:16 * VW].rearrange("p (m w) -> p m w", w=VW)
                    dve.reciprocal(rinv[:, f, :], pv[:, :, 16]).then_inc(rsum_inv, 1)
                    if f == 0:
                        wait(dve, x1hi_made, 4 * i)
                        wait(dve, x1lo_made, 4 * i)
                        wait(dve, xb_made, 4 * i)
                    dve.wait_ge(rsum_inv, 2 * n + f + 1)
                    dve.tensor_tensor(x1[:, u, 256 * f:256 * f + 256].rearrange("p (m w) -> p m w", w=16),
                                      pv[:, :, 0:16],
                                      rinv[:, f, :].rearrange("p (m o) -> p m o", o=1).broadcast_to([128, 16, 16]),
                                      ALU.mult).then_inc(norm_taken, 1)

            def x1_low(i, u):
                n = 4 * i + u
                dve.wait_ge(x1hi_made, n + 1)
                dve.tensor_tensor(x1_lo[u], x1[:, u, :], x1_hi[u].bitcast(F32),
                                  ALU.subtract).then_inc(x1lo_made, 1)

            def find_within(i):
                dve.wait_ge(tables_made, 2 * i + 2)
                for c in range(LB):
                    dve.tensor_scalar(within[:, c, :], seqg[:, :], con("chan")[:, c:c + 1], None,
                                      ALU.is_gt).then_inc(within_made, 1)

            def c2_values(i, u):
                n = 4 * i + u
                rows = c2s[:, u % 2, :].rearrange("p (m s) -> p m s", s=T)
                wait(dve, c2lo_made, n - 1)
                wait(dve, small_done, n - 1)
                dve.wait_ge(c2_done, n + 1)
                dve.tensor_tensor(rows, ps[u % 2][:, :].rearrange("p (m s) -> p m s", s=T),
                                  par("b2").rearrange("p (o s) -> p o s", o=1).broadcast_to([128, 16, T]),
                                  ALU.add).then_inc(c2_biased, 1)
                if u == 0:
                    dve.wait_ge(within_made, 4 * i + 4)
                dve.wait_ge(c2_biased, n + 1)
                rows4 = c2s[:, u % 2, :].rearrange("p (c b s) -> p c b s", c=LB, s=T)
                dve.tensor_tensor(rows4, rows4, within[:, :, 4 * u:4 * u + 4].rearrange("p c (b o) -> p c b o", o=1)
                                  .broadcast_to([128, LB, 4, T]), ALU.mult).then_inc(c2_masked, 1)

            def c2_low(i, u):
                n = 4 * i + u
                dve.wait_ge(c2hi_made, n + 1)
                dve.tensor_tensor(c2T_lo[:, u % 2, :, :], c2s[:, u % 2, :].rearrange("p (c n) -> p c n", c=LB),
                                  c2T_hi[:, u % 2, :, :].bitcast(F32), ALU.subtract).then_inc(c2lo_made, 1)

            def split_lo(j):
                for l in range(LB):
                    dve.wait_ge(yhi_made, LB * j + l + 1)
                    dve.tensor_tensor(y_lo[:, l, :], yG[:, l, j, :], y_hi[:, l, :].bitcast(F32),
                                      ALU.subtract).then_inc(ylo_made, 1)

            NR = 12

            def route(i):
                k = [0]

                def r(ins):
                    k[0] += 1
                    ins.then_inc(router_step, 1)
                    dve.wait_ge(router_step, NR * i + k[0])

                def t3(x):
                    return x.rearrange("p (u e) -> p u e", u=NU)

                z, ki, ci_, su, sz = (rt[:, m, :] for m in range(5))
                kz, tau = rt[:, 5, 0:NU], rt[:, 6, 0:NU]
                G = pair[:, 0, :].rearrange("p (m j) -> p m j", j=NEXP)
                GZ = pair[:, 1, :].rearrange("p (m j) -> p m j", j=NEXP)

                def ui(x):
                    return x.rearrange("p (m o) -> p m o", o=1).broadcast_to([128, NU * NEXP, NEXP])

                def uj(x):
                    return x.rearrange("p (u o e) -> p u o e", u=NU, o=1).broadcast_to([128, NU, NEXP, NEXP])

                def u4(x):
                    return x.rearrange("p (u i) j -> p u i j", u=NU)

                dve.wait_ge(small_taken, 4 * i + 4)
                r(dve.tensor_tensor(t3(z), hsm[:, :, 0:NEXP],
                                    par("brout").rearrange("p (o e) -> p o e", o=1).broadcast_to([128, NU, NEXP]),
                                    ALU.add))
                r(dve.tensor_tensor(u4(G), uj(z), u4(ui(z)), ALU.is_ge))
                r(dve.tensor_tensor(u4(GZ), u4(G), uj(z), ALU.mult))
                r(dve.tensor_reduce(ki, G, AX, ALU.add))
                r(dve.tensor_reduce(ci_, GZ, AX, ALU.add))
                r(dve.tensor_tensor(su, z, ki, ALU.mult))
                r(dve.scalar_tensor_tensor(out=su, in0=su, scalar=1.0, in1=ci_, op0=ALU.add, op1=ALU.is_gt))
                r(dve.tensor_tensor(sz, su, z, ALU.mult))
                r(dve.tensor_reduce(kz, t3(su), AX, ALU.add))
                r(dve.tensor_reduce(tau, t3(sz), AX, ALU.add))
                r(dve.reciprocal(kz, kz))
                r(dve.scalar_tensor_tensor(out=tau, in0=tau, scalar=-1.0, in1=kz, op0=ALU.add, op1=ALU.mult))
                assert k[0] == NR

            def weigh(i):
                z, zt, tau = rt[:, 0, :], rt[:, 7, :], rt[:, 6, 0:NU]
                dve.tensor_tensor(zt.rearrange("p (u e) -> p u e", u=NU), z.rearrange("p (u e) -> p u e", u=NU),
                                  tau.rearrange("p (u o) -> p u o", o=1).broadcast_to([128, NU, NEXP]),
                                  ALU.subtract).then_inc(row_zt, 1)
                dve.wait_ge(row_zt, 2 * i + 1)
                dve.tensor_scalar(zt, zt, 0.0, None, ALU.max).then_inc(row_zt, 1)
                wait(dve, hwT_done, i)
                dve.wait_ge(row_zt, 2 * i + 2)
                dve.tensor_tensor(hw[:, :, :].rearrange("p u (e r) -> p u e r", e=NEXP),
                                  hsm[:, :, NEXP:136].rearrange("p u (e r) -> p u e r", e=NEXP),
                                  zt.rearrange("p (u e o) -> p u e o", u=NU, o=1).broadcast_to([128, NU, NEXP, RANK]),
                                  ALU.mult).then_inc(hw_made, 1)

            def hw_low(i):
                dve.wait_ge(hwT_hi, i + 1)
                dve.tensor_tensor(hwT[1], ps[4][:, :].rearrange("p (u n) -> p u n", u=NU), hwT[0].bitcast(F32),
                                  ALU.subtract).then_inc(hwT_lo, 1)

            def final(i, u):
                n = 4 * i + u
                dve.wait_ge(out_done, n + 1)
                dve.wait_ge(xb_made, n + 1)
                dve.tensor_tensor(xg[:, u, :], [ps[2], ps[3], ps[6], ps[7]][u][:, :], xg[:, u, :],
                                  ALU.add).then_inc(out_taken, 1)

            def group(i, last=False):
                def V(u):
                    if not last:
                        take_v(i + 1, u)
                soft_ = soft_masked if last else soft
                soft_(i, 1); normalise(i, 0); V(0); turn_p(i, 1)
                soft_(i, 2); normalise(i, 1); V(1); turn_p(i, 2)
                soft_(i, 3); normalise(i, 2); V(2); x1_low(i, 0); turn_p(i, 3)
                V(3)
                x1_low(i, 1)
                normalise(i, 3)
                x1_low(i, 2)
                find_within(i)
                x1_low(i, 3)
                for u in range(NU):
                    c2_values(i, u)
                    if u:
                        c2_low(i, u - 1)
                    if not last and u < 2:
                        spread_q(i + 1, True, (u,))
                c2_low(i, NU - 1)
                route(i)
                weigh(i)
                hw_low(i)
                if not last:
                    soft(i + 1, 0)
                final(i, 0); final(i, 1)
                if not last:
                    turn_p(i + 1, 0)
                final(i, 2); final(i, 3)

            split_lo(0)
            dve.wait_ge(thi_made, 32)
            dve.wait_ge(tlo_made, 32)
            dve.memset(kbd[:, :, :, :], 0.0).then_inc(preset, 1)
            dve.wait_ge(kpad_in, 16 * 5)
            dve.memset(v_st[:, :, :, :], 1.0).then_inc(v_ones, 1)
            dve.wait_ge(v_ones, 1)
            take_v(0, 0); take_v(0, 1)
            spread_q(0, False)
            take_v(0, 2); take_v(0, 3)
            split_lo(1)
            dve.wait_ge(ylo_made, 2 * LB)
            soft(0, 0); turn_p(0, 0)
            group(0)
            with dve.Fori(1, 7) as i:
                group(i)
            group(7, last=True)


def kernel(x, itok_B_78_3631, itok_B_0_7, itok_B_2182_4065, _lenS, L0_cond_log_dt, L0_cond_C, L0_cond_log_A_real,
           L0_cond_A_imag, L0_cond_D, L0_attn_Wq, L0_attn_bq, L0_attn_Wk, L0_attn_bk, L0_attn_Wv, L0_attn_bv,
           L0_cond2_W_sess, L0_cond2_b_sess, L0_cond2_W2, L0_cond2_b2, L0_ffn_W_base, L0_ffn_b_base,
           L0_ffn_W_router, L0_ffn_b_router, L0_ffn_lora_A, L0_ffn_lora_B):
    import concourse.bacc as _bacc
    from concourse import mybir as _mybir
    from concourse.bass_utils import run_bass_kernel_spmd as _run

    c_ = np.ascontiguousarray
    f4 = np.float32
    x = np.asarray(x)
    pi = np.arange(C).reshape(2, 2, 2, 4, 16).transpose(1, 3, 0, 2, 4).reshape(-1)

    def rows(a, n=128):
        return np.broadcast_to(np.asarray(a).reshape(1, -1), (n, np.asarray(a).size))

    def dup(a):
        t = np.asarray(a).T
        return np.concatenate([t, t], 0)

    xT = c_(x.reshape(B, T, LB, 128)[:, :, :, ::-1].transpose(1, 3, 2, 0).reshape(T, 128, C))
    xN = c_(x[:, :, pi].reshape(NG, NU, 4 * T, C).transpose(0, 2, 1, 3))
    Cm = np.asarray(L0_cond_C)
    bq = np.asarray(L0_attn_bq).reshape(4, 128).T
    bk = np.asarray(L0_attn_bk).reshape(2, 128).T
    bs = np.asarray(L0_cond2_b_sess).T
    pk = c_(np.concatenate([bq, bk, rows(L0_cond2_b2), rows(L0_ffn_b_router),
                            rows(np.asarray(L0_attn_bv).reshape(2, 2, 4, 16).transpose(1, 0, 2, 3)),
                            rows(np.asarray(L0_ffn_b_base)[pi])], 1))
    p = np.arange(128)
    ri = p // 64
    quarter = np.stack([1 - ri, 1 + ri, 2 + ri], 1).astype(np.float64)
    key, t = np.arange(T)[None, :], (p % T)[:, None]
    skip = np.zeros((4, 32, 8), f4)
    skip[:, 0, :] = np.asarray(L0_cond_D).reshape(8, 4).T
    skip = skip.reshape(128, 8)
    early = c_(np.concatenate([
        rows(L0_cond_log_dt), dup(L0_cond_log_A_real), dup(L0_cond_A_imag), dup(Cm[..., 0]), dup(Cm[..., 1]),
        skip, np.concatenate([bs, bs], 0), (quarter / 4).astype(f4), (quarter * (np.pi / 2)).astype(f4),
        (PI_SAFE - quarter * (np.pi / 2)).astype(f4), (-PI_SAFE - quarter * (np.pi / 2)).astype(f4),
        (p[:, None] + 128 * np.arange(LB)[None, :]).astype(f4), (p % 32)[:, None].astype(f4),
        rows(np.arange(KK, dtype=f4)), rows(KK * np.arange(KI, dtype=f4))], 1))
    cst = c_(np.concatenate([
        (p // 64)[:, None] == np.arange(2)[None, :], (p // 32)[:, None] == np.arange(4)[None, :],
        np.where(key <= t, 0.0, -1e30), pi.reshape(LB, 128).T, np.eye(128)], 1).astype(f4))
    sid = np.asarray(itok_B_0_7)

    def by_bc(a):
        return np.repeat(np.asarray(a).reshape(32, 4).T, T, 0)

    ints = c_(np.concatenate([rows(itok_B_78_3631), by_bc(sid), by_bc(_lenS), rows(itok_B_2182_4065),
                              np.repeat(sid.reshape(64, 2).T, HID, 0)], 1))

    def blocks(w):
        return c_(np.asarray(w).reshape(LB, 128, -1).transpose(1, 0, 2))

    wq = blocks(np.asarray(L0_attn_Wq).T)
    wk = blocks(np.asarray(L0_attn_Wk).T)
    wv = blocks(np.asarray(L0_attn_Wv).reshape(2, 2, 4, 16, C).transpose(1, 0, 2, 3, 4).reshape(256, C).T)
    wsess = c_(np.asarray(L0_cond2_W_sess).transpose(1, 0, 2))
    wbase = blocks(np.asarray(L0_ffn_W_base)[pi][:, pi].T)
    la = np.asarray(L0_ffn_lora_A)[:, pi].transpose(1, 0, 2).reshape(C, 128)
    wsmall = blocks(np.concatenate([np.asarray(L0_ffn_W_router)[:, pi].T, la], 1))
    lorab = c_(np.asarray(L0_ffn_lora_B).reshape(128, C)[:, pi])

    nc = _bacc.Bacc("TRN2", target_bir_lowering=False, num_devices=1)
    arrays, args = {}, []
    for name, a in (("xT", xT), ("xN", xN), ("early", early), ("pk", pk), ("cst", cst), ("ints", ints), ("wq", wq), ("wk", wk),
                    ("wv", wv), ("wsess", wsess), ("w2", c_(np.asarray(L0_cond2_W2))), ("wbase", wbase),
                    ("wsmall", wsmall), ("lorab", lorab)):
        arrays[name] = a
        args.append(nc.dram_tensor(name, a.shape, _mybir.dt.from_np(a.dtype), kind="ExternalInput").ap())
    out = nc.dram_tensor("out", (NG, 128, NU, C), _mybir.dt.float32, kind="ExternalOutput").ap()
    kpad = nc.dram_tensor("kpad", (32, PADW), _mybir.dt.float32, kind="Internal").ap()
    yspill = nc.dram_tensor("yspill", (NG, 128, LB, TOK), _mybir.dt.float32, kind="Internal").ap()
    vrows = nc.dram_tensor("vrows", (NG, NU, 4, T, 2, 8 * VW), _mybir.dt.float32, kind="Internal").ap()
    adaln_attn_ffn(nc, *args, out, kpad, yspill, vrows)
    r = _run(nc, [arrays], core_ids=[0])
    o = np.asarray(r.results[0]["out"]).transpose(0, 2, 1, 3).reshape(B, T, C)
    inv = np.empty_like(pi)
    inv[pi] = np.arange(C)
    return c_(o[:, :, inv])
```
